# Optimizing a Trainium2 kernel written in Bass

```python
import numpy as np
import jax
import jax.numpy as jnp

def _softmax(x, axis=-1):
    return jax.nn.softmax(x, axis=axis)

def _gelu(x):
    return jax.nn.gelu(x, approximate=True)

def _silu(x):
    return jax.nn.silu(x)

def _sigmoid(x):
    return jax.nn.sigmoid(x)

def _layernorm(x, axis=-1, eps=1e-05):
    m = jnp.mean(x, axis=axis, keepdims=True)
    v = jnp.var(x, axis=axis, keepdims=True)
    return (x - m) / jnp.sqrt(v + eps)

def _scatter_add(tgt, idx, src, axis=0):
    return tgt.at[idx].add(src)

def _segment_sum(src, seg, n):
    return jax.ops.segment_sum(src, seg, n)
kernel_name = 'mk_decoder_preln_d1_seqx_r8_6e700e'

def setup_inputs(seed: int=0):
    np.random.seed(seed)
    _w = jnp.asarray

    def _rec_inputs():
        import jax
        import jax.numpy as jnp
        _rk = jax.random.key(seed)
        x = -0.0003929 + 0.9999 * jax.random.normal(jax.random.fold_in(_rk, 1), (2, 512, 128), jnp.float32)
        _lenS = 512 - jax.random.randint(jax.random.fold_in(_rk, 7), (2,), 0, max(1, 512 // 4) + 1, jnp.int32)
        _lenS2 = 77 - jax.random.randint(jax.random.fold_in(_rk, 8), (2,), 0, max(1, 77 // 4) + 1, jnp.int32)
        _ctx_768P = jax.random.normal(jax.random.fold_in(_rk, 11), (2, 16, 96), jnp.float32)
        _ctx_768c = jax.random.dirichlet(jax.random.fold_in(_rk, 511), 0.3 * jnp.ones((16,), jnp.float32), (2, 77))
        _ctx_768t = jnp.einsum('bsk,bkd->bsd', _ctx_768c, _ctx_768P)
        _ctx_768t = _ctx_768t * jax.lax.rsqrt(jnp.mean(jnp.square(_ctx_768t)) + 1e-12) * 0.953939
        ctx_768 = -0.00055796 + 0.999787 * (_ctx_768t + 0.3 * jax.random.normal(jax.random.fold_in(_rk, 611), (2, 77, 96), jnp.float32))
        return (x, ctx_768)
    x, ctx_768 = _rec_inputs()

    def _L0_attn_setup():
        import jax, jax.numpy as jnp
        import numpy as np
        import math
        B, S, DIM, HEADS = (2, 256, 128, 16)

        def _alibi_slopes(n_heads):

            def pow2_slopes(n):
                start = 2 ** (-2 ** (-(math.log2(n) - 3)))
                return [start * start ** i for i in range(n)]
            if math.log2(n_heads).is_integer():
                slopes = pow2_slopes(n_heads)
            else:
                closest = 2 ** math.floor(math.log2(n_heads))
                slopes = pow2_slopes(closest)
                slopes += pow2_slopes(2 * closest)[0::2][:n_heads - closest]
            return np.asarray(slopes, dtype=np.float32).reshape(n_heads, 1, 1)
        key = jax.random.key(seed)
        k1, k2, k3 = jax.random.split(key, 3)
        x = jax.random.normal(k1, (B, S, DIM), dtype=jnp.float32)
        W_qkv = jax.random.normal(k2, (3 * DIM, DIM), dtype=jnp.float32) * 0.02
        W_o = jax.random.normal(k3, (DIM, DIM), dtype=jnp.float32) * 0.02
        return {'x': x, 'W_qkv': W_qkv, 'W_o': W_o}
    _L0_attn_all = _L0_attn_setup()
    _L0_attn_in = {k: v for k, v in _L0_attn_all.items() if k in ('W_qkv', 'W_o')}
    del _L0_attn_all

    def _L0_xattn_setup():
        import jax, jax.numpy as jnp
        import numpy as np
        IMAGE_DIM = 128
        TEXT_DIM = 96
        NUM_HEADS = 16
        HEAD_DIM = IMAGE_DIM // NUM_HEADS
        key = jax.random.key(seed)
        ks = jax.random.split(key, 14)
        B, N, M = (4, 512, 64)
        s_img = 1.0 / np.sqrt(IMAGE_DIM)
        s_txt = 1.0 / np.sqrt(TEXT_DIM)
        s_ff = 1.0 / np.sqrt(2 * IMAGE_DIM)
        return {'x': jax.random.normal(ks[0], (B, N, IMAGE_DIM), jnp.float32), 'y': jax.random.normal(ks[1], (B, M, TEXT_DIM), jnp.float32), 'Wq': jax.random.normal(ks[2], (IMAGE_DIM, IMAGE_DIM), jnp.float32) * s_img, 'bq': jax.random.normal(ks[3], (IMAGE_DIM,), jnp.float32) * s_img, 'Wk': jax.random.normal(ks[4], (TEXT_DIM, IMAGE_DIM), jnp.float32) * s_txt, 'bk': jax.random.normal(ks[5], (IMAGE_DIM,), jnp.float32) * s_txt, 'Wv': jax.random.normal(ks[6], (TEXT_DIM, IMAGE_DIM), jnp.float32) * s_txt, 'bv': jax.random.normal(ks[7], (IMAGE_DIM,), jnp.float32) * s_txt, 'W1': jax.random.normal(ks[8], (IMAGE_DIM, 2 * IMAGE_DIM), jnp.float32) * s_img, 'b1': jax.random.normal(ks[9], (2 * IMAGE_DIM,), jnp.float32) * s_img, 'W2': jax.random.normal(ks[10], (2 * IMAGE_DIM, IMAGE_DIM), jnp.float32) * s_ff, 'b2': jax.random.normal(ks[11], (IMAGE_DIM,), jnp.float32) * s_ff}
    _L0_xattn_all = _L0_xattn_setup()
    _L0_xattn_in = {k: v for k, v in _L0_xattn_all.items() if k in ('Wq', 'bq', 'Wk', 'bk', 'Wv', 'bv', 'W1', 'b1', 'W2', 'b2')}
    del _L0_xattn_all

    def _L0_ffn_setup():
        import jax, jax.numpy as jnp
        import numpy as np
        NUM_EXPERTS = 8
        EXPERT_CAPACITY = 2.0
        key = jax.random.key(seed)
        k1, k2, k3, k4 = jax.random.split(key, 4)
        B, T, C, H, E = (4, 512, 128, 512, NUM_EXPERTS)
        x = jax.random.normal(k1, (B, T, C), jnp.float32)
        gate_w = jax.random.normal(k2, (C, E), jnp.float32) * 0.02
        w1 = jax.random.normal(k3, (E, C, H), jnp.float32) * 0.02
        w2 = jax.random.normal(k4, (E, H, C), jnp.float32) * 0.02
        return {'x': x, 'gate_w': gate_w, 'w1': w1, 'w2': w2}
    _L0_ffn_all = _L0_ffn_setup()
    _L0_ffn_in = {k: v for k, v in _L0_ffn_all.items() if k in ('gate_w', 'w1', 'w2')}
    del _L0_ffn_all
    return {'x': x, 'ctx_768': ctx_768, 'L0_attn_W_qkv': _L0_attn_in['W_qkv'], 'L0_attn_W_o': _L0_attn_in['W_o'], 'L0_xattn_Wq': _L0_xattn_in['Wq'], 'L0_xattn_bq': _L0_xattn_in['bq'], 'L0_xattn_Wk': _L0_xattn_in['Wk'], 'L0_xattn_bk': _L0_xattn_in['bk'], 'L0_xattn_Wv': _L0_xattn_in['Wv'], 'L0_xattn_bv': _L0_xattn_in['bv'], 'L0_xattn_W1': _L0_xattn_in['W1'], 'L0_xattn_b1': _L0_xattn_in['b1'], 'L0_xattn_W2': _L0_xattn_in['W2'], 'L0_xattn_b2': _L0_xattn_in['b2'], 'L0_ffn_gate_w': _L0_ffn_in['gate_w'], 'L0_ffn_w1': _L0_ffn_in['w1'], 'L0_ffn_w2': _L0_ffn_in['w2']}

def reference(x, ctx_768, L0_attn_W_qkv, L0_attn_W_o, L0_xattn_Wq, L0_xattn_bq, L0_xattn_Wk, L0_xattn_bk, L0_xattn_Wv, L0_xattn_bv, L0_xattn_W1, L0_xattn_b1, L0_xattn_W2, L0_xattn_b2, L0_ffn_gate_w, L0_ffn_w1, L0_ffn_w2):
    import jax
    import jax.numpy as jnp

    def _L0_attn_ref(x, W_qkv, W_o):
        import jax, jax.numpy as jnp
        import numpy as np
        import math
        B, S, DIM, HEADS = (2, 256, 128, 16)

        def _alibi_slopes(n_heads):

            def pow2_slopes(n):
                start = 2 ** (-2 ** (-(math.log2(n) - 3)))
                return [start * start ** i for i in range(n)]
            if math.log2(n_heads).is_integer():
                slopes = pow2_slopes(n_heads)
            else:
                closest = 2 ** math.floor(math.log2(n_heads))
                slopes = pow2_slopes(closest)
                slopes += pow2_slopes(2 * closest)[0::2][:n_heads - closest]
            return np.asarray(slopes, dtype=np.float32).reshape(n_heads, 1, 1)
        b, s, d = x.shape
        h = HEADS
        hd = d // h
        scale = hd ** (-0.5)
        qkv = x @ W_qkv.T
        q, k, v = jnp.split(qkv, 3, axis=-1)
        q = q.reshape(b, s, h, hd).transpose(0, 2, 1, 3)
        k = k.reshape(b, s, h, hd).transpose(0, 2, 1, 3)
        v = v.reshape(b, s, h, hd).transpose(0, 2, 1, 3)
        scores = jnp.einsum('bhqd,bhkd->bhqk', q, k) * scale
        pos = jnp.arange(s)
        rel = (pos[None, :] - pos[:, None]).astype(scores.dtype)
        slopes = jnp.asarray(_alibi_slopes(h))
        scores = scores - slopes * rel
        causal_mask = pos[None, :] > pos[:, None]
        scores = jnp.where(causal_mask, jnp.finfo(scores.dtype).min, scores)
        weights = jax.nn.softmax(scores, axis=-1)
        out = jnp.einsum('bhqk,bhkd->bhqd', weights, v)
        out = out.transpose(0, 2, 1, 3).reshape(b, s, d)
        return out @ W_o.T

    def _L0_xattn_ref(x, y, Wq, bq, Wk, bk, Wv, bv, W1, b1, W2, b2):
        import jax, jax.numpy as jnp
        import numpy as np
        IMAGE_DIM = 128
        TEXT_DIM = 96
        NUM_HEADS = 16
        HEAD_DIM = IMAGE_DIM // NUM_HEADS
        B, N, _ = x.shape
        M = y.shape[1]
        q = (x @ Wq + bq).reshape(B, N, NUM_HEADS, HEAD_DIM)
        k = (y @ Wk + bk).reshape(B, M, NUM_HEADS, HEAD_DIM)
        v = (y @ Wv + bv).reshape(B, M, NUM_HEADS, HEAD_DIM)
        scale = 1.0 / np.sqrt(HEAD_DIM)
        scores = jnp.einsum('bnhd,bmhd->bhnm', q, k) * scale
        attn = jax.nn.softmax(scores, axis=-1)
        out = jnp.einsum('bhnm,bmhd->bnhd', attn, v).reshape(B, N, IMAGE_DIM)
        h = jax.nn.relu(out @ W1 + b1)
        return h @ W2 + b2

    def _L0_ffn_ref(x, gate_w, w1, w2):
        import jax, jax.numpy as jnp
        import numpy as np
        NUM_EXPERTS = 8
        EXPERT_CAPACITY = 2.0
        B, T, C = x.shape
        E = gate_w.shape[1]
        cap = int(EXPERT_CAPACITY * T / E)
        scores = jnp.einsum('BTC,CE->BTE', x, gate_w)
        probs = jax.nn.softmax(scores, axis=-1)
        probs_et = jnp.transpose(probs, (0, 2, 1))
        top_p, top_idx = jax.lax.top_k(probs_et, cap)
        xin = jnp.take_along_axis(x[:, None, :, :], top_idx[..., None], axis=2)
        h = jax.nn.gelu(jnp.einsum('BElC,ECH->BElH', xin, w1), approximate=False)
        y = jnp.einsum('BElH,EHC->BElC', h, w2)
        y = y * top_p[..., None]
        b_idx = jnp.arange(B)[:, None, None]
        out = jnp.zeros((B, T, C), x.dtype).at[b_idx, top_idx].add(y)
        return out
    x = x + _L0_attn_ref(_layernorm(x, axis=-1), L0_attn_W_qkv, L0_attn_W_o)
    x = x + _L0_xattn_ref(_layernorm(x, axis=-1), ctx_768, L0_xattn_Wq, L0_xattn_bq, L0_xattn_Wk, L0_xattn_bk, L0_xattn_Wv, L0_xattn_bv, L0_xattn_W1, L0_xattn_b1, L0_xattn_W2, L0_xattn_b2)
    x = x + _L0_ffn_ref(_layernorm(x, axis=-1), L0_ffn_gate_w, L0_ffn_w1, L0_ffn_w2)
    return x

_drawn_inputs = setup_inputs


def setup_inputs(seed=0):
    import zlib

    import numpy as np

    out = dict(_drawn_inputs(seed))
    spreads = {}
    factors = {'L0_attn_W_qkv': 3.579,
     'L0_attn_W_o': 4.386,
     'L0_xattn_bq': 4.03,
     'L0_xattn_bk': 8.0,
     'L0_ffn_gate_w': 5.717,
     'L0_ffn_w1': 5.101,
     'L0_ffn_w2': 5.014}
    for name, (base, spread) in spreads.items():
        noise = np.random.default_rng([zlib.crc32(name.encode()), seed]).standard_normal(out[name].shape)
        drawn = base * np.exp(spread * noise) if base else spread * noise
        out[name] = jnp.asarray(drawn.astype(out[name].dtype))
    for name, factor in factors.items():
        out[name] = (out[name] * factor).astype(out[name].dtype)
    return out
```

```python
from contextlib import ExitStack

import numpy as np

import concourse.bass as bass
from concourse import mybir

F32 = mybir.dt.float32
BF16 = mybir.dt.bfloat16
U32 = mybir.dt.uint32
ALU = mybir.AluOpType
ACT = mybir.ActivationFunctionType
AX = mybir.AxisListType

P = 128
B, S, C, H = 2, 512, 128, 16
HD = C // H
NT = S // P
M, CT = 77, 96
MP = 80
E, CAP, FF = 8, 2 * S // 8, 512
NC = FF // P
G = 4
NG = H // G
SCALE = float(np.float32(HD ** -0.5))
EPS = 1e-5

PARTS = 3
SLOT_ROWS = PARTS * PARTS * HD
ALIBI = SLOT_ROWS
MAXROW = P - 2
VW = 32


def max_units(kind):
    if kind == "cross":
        return [(t, tuple(range(G)), M) for t in range(NT)]
    return ([(3, (h,), 4 * P) for h in range(G)] + [(2, (h,), 3 * P) for h in range(G)]
            + [(1, (0, 1), 2 * P), (1, (2, 3), 2 * P), (0, (0, 1, 2, 3), P)])


def exp_units(kind):
    pairs = []
    for a in (0, 2):
        if kind == "cross":
            pairs.append([(S * h, S, [(h, 0, 0, 0)]) for h in (a, a + 1)])
            continue
        units = []
        for h in (a, a + 1):
            units.append((2 * S * h, S, [(h, 0, 0, 0)]))
            units.append((2 * S * h + S, S, [(h, 1, 0, 1), (h, 3, 3 * P, 3)]))
        units.append((2 * S * G + S * (a // 2), S, [(a, 2, 0, 2), (a + 1, 2, 2 * P, 2)]))
        pairs.append(units)
    return pairs


def decoder_block(nc, x, ctxT, wqkvT, woT, wq, bq, wk, bk, wv, bv, w1, b1, w2, b2, gate_w, mw1, mw2,
                  alibi, ones_rows, ident, iota1, out):
    groups = [("self", b, g) for b in range(B) for g in range(NG)] + \
             [("cross", b, g) for b in range(B) for g in range(NG)]
    NGR = len(groups)
    mx_first, st_first = [0], [0]
    for kind, _, _ in groups:
        mx_first.append(mx_first[-1] + len(max_units(kind)))
        st_first.append(st_first[-1] + sum(len(p) for p in exp_units(kind)))
    MXB, STB = 3, 3
    LEAD = 2

    ctx = ExitStack()
    with ctx:
        def sb(name, shape, dt=F32):
            return ctx.enter_context(nc.sbuf_tensor(name, shape, dt))

        def sem(name):
            return ctx.enter_context(nc.semaphore(name))

        ps = [ctx.enter_context(nc.psum_tensor(f"bank{i}", [P, 512], F32)) for i in range(8)]
        mx_banks = [ps[2], ps[3], ps[6]]
        st_banks = [ps[4], ps[5], ps[7]]
        pv_bank, tp_bank = ps[0], ps[1]

        x_sb = sb("x_sb", [P, B, NT, C])
        xn = sb("xn", [P, B, NT, C])
        xnT = sb("xnT", [P, B, S])
        stats = sb("stats", [P, NT, 6])
        mv = sb("mv", [P, B * NT, 2])
        veps = sb("veps", [P, B * NT])
        rstd = sb("rstd", [P, B * NT])
        neghalf = sb("neghalf", [P, NT])
        wqkvT_sb = sb("wqkvT_sb", [P, 3 * C])
        woT_sb = sb("woT_sb", [P, C])
        wq_sb = sb("wq_sb", [P, C])
        wk_sb = sb("wk_sb", [CT, C])
        wv_sb = sb("wv_sb", [CT, C])
        w1_sb = sb("w1_sb", [P, 2 * C])
        w2_sb = sb("w2_sb", [P, 2, C])
        bq_sb = sb("bq_sb", [P, 1])
        bk_sb = sb("bk_sb", [P, 1])
        b1_sb = sb("b1_sb", [P, 2])
        bv_sb = sb("bv_sb", [M, C])
        b2_sb = sb("b2_sb", [P, C])
        gw_sb = sb("gw_sb", [P, E])
        ctxT_sb = sb("ctxT_sb", [CT, B, MP])
        ident_sb = sb("ident_sb", [P, P])
        identb = sb("identb", [P, P], BF16)
        maskb = sb("maskb", [P, P], BF16)
        iota_sb = sb("iota_sb", [P, P])
        mw1_sb = sb("mw1_sb", [P, E, FF])
        mw2_sb = sb("mw2_sb", [P, E, NC, C])
        full = sb("full", [P, S])
        rest = sb("rest", [P, S])
        parts = [sb(f"parts{i}", [P, PARTS, S], BF16) for i in range(2)]
        Qs = [sb(f"Qs{b}", [P, H, S], BF16) for b in range(B)]
        Ks = [sb(f"Ks{b}", [P, H, S], BF16) for b in range(B)]
        K2s = sb("K2s", [P, H, B, MP], BF16)
        Vs = [sb(f"Vs{b}", [P, NT, H, VW]) for b in range(B)]
        V2s = sb("V2s", [M, B, H, VW])
        prob = [sb(f"prob{i}", [P, 5 * 2 * S]) for i in range(2)]
        nmax = sb("nmax", [P, NT, G])
        nmp = [sb(f"nmp{i}", [P, NT, 2, G], BF16) for i in range(2)]
        nmT = [sb(f"nmT{i}", [2 * G, S], BF16) for i in range(2)]
        oT = sb("oT", [P, S])
        rden = sb("rden", [P, NT, G])
        on = [sb(f"on{b}", [P, NT, C]) for b in range(B)]
        onT = sb("onT", [P, B, S])
        h1 = Ks[0][:].rearrange("p h s -> p (h s)").bitcast(F32)[:, 0:B * 2 * S].rearrange("p (b j s) -> p b j s", b=B, j=2)
        onehot = [prob[0][:, i * B * S:(i + 1) * B * S].rearrange("p (b t s) -> p b t s", b=B, t=NT) for i in range(2)]
        weighted = [prob[0][:, (2 + i) * B * S:(3 + i) * B * S].rearrange("p (b t s) -> p b t s", b=B, t=NT)
                    for i in range(2)]
        hidden = prob[0][:, 4 * B * S:5 * B * S].rearrange("p (c n) -> p c n", c=NC)
        scatter = [prob[1][:, i * B * S:(i + 1) * B * S].rearrange("p (b t s) -> p b t s", b=B, t=NT)
                   for i in range(2)]
        xin = prob[1][:, 2 * B * S:2 * B * S + B * CAP]
        y_sb = prob[1][:, 2 * B * S + B * CAP:2 * B * S + 2 * B * CAP].rearrange("p (b c) -> p b c", b=B)
        NB8 = NT * B
        gmax = sb("gmax", [P, NB8])
        gsum = sb("gsum", [P, NB8])
        pr = sb("pr", [P, NB8, E])
        late = Ks[1][:].rearrange("p h s -> p (h s)").bitcast(F32)[0:B * E]
        work, sel, slot = (late[:, i * S:(i + 1) * S] for i in range(3))
        ones = sb("ones", [B * E, S])
        top8 = sb("top8", [B * E, 8])
        slT = sb("slT", [P, NT, B * E])

        q_scr = [nc.dram_tensor(f"q_scr{i}", (PARTS, HD, H, S), BF16, kind="Internal").ap() for i in range(2 * B)]
        k_scr = [nc.dram_tensor(f"k_scr{b}", (PARTS, HD, H, S), BF16, kind="Internal").ap() for b in range(B)]
        k2_scr = nc.dram_tensor("k2_scr", (PARTS, HD, H, B * MP), BF16, kind="Internal").ap()

        s_x = [sem(f"s_x{b}") for b in range(B)]
        s_w = sem("s_w")
        s_moew = sem("s_moew")
        s_const = sem("s_const")
        s_pad = sem("s_pad")
        s_rows = sem("s_rows")
        s_vpad = sem("s_vpad")
        s_dve = sem("s_dve")
        s_var = sem("s_var")
        s_rstd = sem("s_rstd")
        s_xn = sem("s_xn")
        s_xnTp = sem("s_xnTp")
        s_xnT = sem("s_xnT")
        s_proj = sem("s_proj")
        s_parts = sem("s_parts")
        s_scr = sem("s_scr")
        s_stack = [sem(f"s_stack{n}") for n in range(NGR)]
        s_k2 = sem("s_k2")
        s_v = sem("s_v")
        s_mx = sem("s_mx")
        s_mxfree = sem("s_mxfree")
        s_nmp = sem("s_nmp")
        s_nmTp = sem("s_nmTp")
        s_nmT = sem("s_nmT")
        s_nmrow = [sem(f"s_nmrow{i}") for i in range(2)]
        s_st = sem("s_st")
        s_exp = sem("s_exp")
        s_causal = sem("s_causal")
        s_pv = sem("s_pv")
        s_oT = sem("s_oT")
        s_oTp = sem("s_oTp")
        s_on = sem("s_on")
        s_onTp = sem("s_onTp")
        s_onT = sem("s_onT")
        s_res = sem("s_res")
        s_h1p = sem("s_h1p")
        s_h1 = sem("s_h1")
        s_gate = sem("s_gate")
        s_gz = sem("s_gz")
        s_gexp = sem("s_gexp")
        s_pr = sem("s_pr")
        s_prT = sem("s_prT")
        s_slot = sem("s_slot")
        s_slotT = sem("s_slotT")
        s_onehot = sem("s_onehot")
        s_weighted = sem("s_weighted")
        s_gather = sem("s_gather")
        s_xin = sem("s_xin")
        s_hid = sem("s_hid")
        s_gelu = sem("s_gelu")
        s_yp = sem("s_yp")
        s_y = sem("s_y")
        s_scp = sem("s_scp")
        s_sc = sem("s_sc")
        s_comb = sem("s_comb")
        s_fin = sem("s_fin")
        s_out = sem("s_out")

        NW = 2 + 13 + 2
        def proj_qkv(b, i):
            return 3 + 3 * b + i

        def proj_q2(b):
            return 2 + 3 * B + 1 + b

        block = ctx.enter_context(nc.Block())

        @block.sync
        def _(sp):
            xv = x.rearrange("b (t p) c -> p b t c", p=P)
            for b in range(B):
                sp.dma_start(x_sb[:, b], xv[:, b]).then_inc(s_x[b], 16)
            sp.wait_ge(s_const, 1)
            for b in range(B):
                sp.dma_start(ctxT_sb[:, b, 0:M], ctxT[:, b, :]).then_inc(s_w, 16)
            for dst, src in ((wqkvT_sb, wqkvT), (wk_sb, wk), (wv_sb, wv), (bk_sb, bk), (ident_sb, ident),
                             (woT_sb, woT), (wq_sb, wq), (bq_sb, bq), (w1_sb, w1), (w2_sb, w2), (b1_sb, b1),
                             (gw_sb, gate_w), (iota_sb, iota1)):
                sp.dma_start(dst[:], src).then_inc(s_w, 16)
            sp.dma_start(bv_sb[:], bv.partition_broadcast(M)).then_inc(s_w, 16)
            sp.dma_start(b2_sb[:], b2.partition_broadcast(P)).then_inc(s_w, 16)
            for b in range(B):
                sp.wait_ge(s_pad, 2 * b + 2)
                sp.dma_start(Ks[b][ALIBI:ALIBI + 3], alibi).then_inc(s_rows, 16)
                sp.dma_start(Ks[b][MAXROW:P], ones_rows[0:2]).then_inc(s_rows, 16)
                sp.dma_start(Qs[b][ALIBI:ALIBI + 3], ones_rows).then_inc(s_rows, 16)
            sp.wait_ge(s_pad, 2 * B + 1)
            sp.dma_start(K2s[MAXROW:P].rearrange("p h b m -> p (h b m)"),
                         ones_rows[0:2].rearrange("p h s -> p (h s)")[:, 0:H * B * MP]).then_inc(s_rows, 16)

            n_split = 0

            def to_scratch(scr, width):
                nonlocal n_split
                sp.wait_ge(s_parts, n_split + 1)
                for p in range(PARTS):
                    sp.dma_start(scr[p].rearrange("d h s -> h d s"), parts[n_split % 2][:, p, 0:width])\
                        .then_inc(s_scr, 16)
                n_split += 1
                sp.wait_ge(s_scr, 16 * PARTS * n_split)

            def stack_k(dst, scr, h0, h1, s):
                for r in range(PARTS):
                    rows = PARTS * HD
                    sp.dma_start(dst[rows * r:rows * r + rows, h0:h1],
                                 scr.rearrange("p d h s -> (p d) h s")[:, h0:h1]).then_inc(s, 16)

            def stack_q(dst, scr, h0, h1, s):
                for p in range(PARTS):
                    for r in range(PARTS):
                        row = HD * (PARTS * p + r)
                        sp.dma_start(dst[row:row + HD, h0:h1], scr[p, :, h0:h1]).then_inc(s, 16)

            to_scratch(k2_scr, B * MP)
            stack_k(K2s[:].rearrange("p h b m -> p h (b m)"), k2_scr, 0, H, s_k2)
            for b in range(B):
                to_scratch(q_scr[b], S)
                to_scratch(k_scr[b], S)
                for g in range(NG):
                    stack_q(Qs[b], q_scr[b], G * g, G * g + G, s_stack[NG * b + g])
                    stack_k(Ks[b], k_scr[b], G * g, G * g + G, s_stack[NG * b + g])
            sp.dma_start(mw1_sb[:], mw1).then_inc(s_moew, 16)
            sp.dma_start(mw2_sb[:], mw2).then_inc(s_moew, 16)

            def negmax_rows(n):
                kind, b, g = groups[n]
                sp.wait_ge(s_nmT, n + 1)
                for i in range(2):
                    sp.dma_start(Qs[b][MAXROW + i:MAXROW + i + 1, G * g:G * g + G],
                                 nmT[n % 2][G * i:G * i + G]).then_inc(s_nmrow[n % 2], 16)

            for n in range(B * NG):
                negmax_rows(n)
            sp.wait_ge(s_st, st_first[B * NG])
            for b in range(B):
                to_scratch(q_scr[B + b], S)
                for g in range(NG):
                    stack_q(Qs[b], q_scr[B + b], G * g, G * g + G, s_stack[B * NG + NG * b + g])
            for n in range(B * NG, NGR):
                negmax_rows(n)
            ov = out.rearrange("b (t p) c -> p b t c", p=P)
            for b in range(B):
                sp.wait_ge(s_fin, b + 1)
                sp.dma_start(ov[:, b], x_sb[:, b]).then_inc(s_out, 16)
            sp.wait_ge(s_out, 16 * B)

        @block.gpsimd
        def _(pool):
            pool.memset(ctxT_sb[:], 0.0).then_inc(s_const, 1)
            pool.memset(neghalf[:], -0.5).then_inc(s_const, 1)
            pool.memset(maskb[:], 0.0).then_inc(s_const, 1)
            pool.memset(ones[:], 1.0).then_inc(s_const, 1)
            pool.wait_ge(s_const, 4)
            pool.affine_select(out=maskb[:], in_=maskb[:], compare_op=ALU.is_ge, fill=-1e30, base=0,
                               pattern=[[-1, P]], channel_multiplier=1).then_inc(s_const, 1)
            pool.memset(V2s[:], 0.0).then_inc(s_vpad, 1)
            pool.wait_ge(s_vpad, 1)
            pool.memset(V2s[:, :, :, HD:HD + 1], 1.0).then_inc(s_vpad, 1)

            def rstd_of(n, b):
                pool.wait_ge(s_var, n + 1)
                pool.tensor_tensor(rstd[:, NT * b:NT * b + NT], veps[:, NT * b:NT * b + NT], neghalf[:],
                                   ALU.pow).then_inc(s_rstd, 1)

            for b in range(B):
                rstd_of(b, b)
            for b in range(B):
                pool.memset(Vs[b][:], 0.0).then_inc(s_vpad, 1)
                pool.wait_ge(s_vpad, 3 + 2 * b)
                pool.memset(Vs[b][:, :, :, HD:HD + 1], 1.0).then_inc(s_vpad, 1)
                pool.wait_ge(s_vpad, 4 + 2 * b)
                for i, t in enumerate((Ks[b], Qs[b])):
                    pool.memset(t[64:P].bitcast(U32), 0).then_inc(s_pad, 1)
                    pool.wait_ge(s_pad, 2 * b + i + 1)
            pool.memset(K2s[64:P].bitcast(U32), 0).then_inc(s_pad, 1)
            pool.wait_ge(s_pad, 2 * B + 1)

            def clear_future_keys(n):
                seq = st_first[n]
                for units in exp_units("self"):
                    for at, width, blocks in units:
                        pool.wait_ge(s_exp, seq + 1)
                        nb, step = len(blocks), max(blocks[-1][2], P)
                        v = prob[n % 2][:, at:at + step * nb].rearrange("p (n s) -> p n s", s=step)[:, :, 0:P]
                        if nb * step > S:
                            v = prob[n % 2][:, at:at + S].rearrange("p (n s) -> p n s", s=P)[:, 0:NT:NT - 1, :]
                        pool.affine_select(out=v, in_=v, compare_op=ALU.is_ge, fill=0.0, base=0,
                                           pattern=[[0, nb], [1, P]], channel_multiplier=-1).then_inc(s_causal, 1)
                        seq += 1

            for n in range(B * NG):
                clear_future_keys(n)
            for ln in (1, 2):
                for b in range(B):
                    rstd_of(B * ln + b, b)

        @block.scalar
        def _(act):
            act.wait_ge(s_proj, 2)
            act.wait_ge(s_vpad, 2)
            for b in range(B):
                act.copy(V2s[:, b, :, 0:HD], ps[1][0:M, b * C:(b + 1) * C].rearrange("p (h d) -> p h d", d=HD))\
                    .then_inc(s_v, 1)
            for b in range(B):
                act.wait_ge(s_xnTp, b + 1)
                act.copy(xnT[:, b], ps[2 + b][:]).then_inc(s_xnT, 1)
            for b in range(B):
                act.wait_ge(s_proj, proj_qkv(b, 2))
                act.wait_ge(s_vpad, 4 + 2 * b)
                act.copy(Vs[b][:, :, :, 0:HD], ps[(6, 1)[b]][:].rearrange("p (t h d) -> p t h d", t=NT, d=HD))\
                    .then_inc(s_v, 1)

            def evict_negmax(n):
                act.wait_ge(s_nmTp, n + 1)
                if n >= 2:
                    act.wait_ge(s_nmrow[n % 2], 32 * (n // 2))
                act.copy(nmT[n % 2][:], tp_bank[:].bitcast(BF16)[0:2 * G, 0:S]).then_inc(s_nmT, 1)

            def exps(n, p):
                kind = groups[n][0]
                rows = P if kind == "self" else M
                units = exp_units(kind)
                seq = st_first[n] + sum(len(u) for u in units[:p])
                for at, width, blocks in units[p]:
                    act.wait_ge(s_st, seq + 1)
                    if n >= 2:
                        act.wait_ge(s_pv, n - 1)
                    act.activation(prob[n % 2][0:rows, at:at + width], st_banks[seq % STB][0:rows, 0:width],
                                   ACT.Exp).then_inc(s_exp, 1)
                    seq += 1

            def evict_pv(n):
                act.wait_ge(s_pv, n + 1)
                if n > 0:
                    act.wait_ge(s_oTp, n)
                act.copy(oT[:], pv_bank[:]).then_inc(s_oT, 1)

            def pipeline(n0, n1):
                for n in range(n0, n0 + LEAD):
                    evict_negmax(n)
                for n in range(n0, n1):
                    exps(n, 0)
                    if n > n0:
                        evict_pv(n - 1)
                    exps(n, 1)
                    if n + LEAD < n1:
                        evict_negmax(n + LEAD)
                evict_pv(n1 - 1)

            pipeline(0, B * NG)
            for b in range(B):
                act.wait_ge(s_xnTp, B + b + 1)
                act.copy(xnT[:, b], ps[2 + 4 * b][:]).then_inc(s_xnT, 1)
            pipeline(B * NG, NGR)
            for b in range(B):
                act.wait_ge(s_h1p, b + 1)
                for j in range(2):
                    act.activation(h1[:, b, j], ps[4 * b + 1 + j][:], ACT.Relu, bias=b1_sb[:, j:j + 1])\
                        .then_inc(s_h1, 1)
            for b in range(B):
                act.wait_ge(s_xnTp, 2 * B + b + 1)
                act.copy(xnT[:, b], ps[4 * b][:]).then_inc(s_xnT, 1)
            act.wait_ge(s_gz, 1)
            act.activation(pr[:], pr[:], ACT.Exp).then_inc(s_gexp, 1)

            def evict_scatter(e):
                act.wait_ge(s_scp, e + 1)
                if e >= 2:
                    act.wait_ge(s_comb, e - 1)
                for b in range(B):
                    act.copy(scatter[e % 2][:, b], ps[6 + b][:].rearrange("p (t s) -> p t s", t=NT)).then_inc(s_sc, 1)

            evict_scatter(0)
            for e in range(E):
                act.wait_ge(s_hid, e + 1)
                for j in range(2):
                    act.activation(hidden[:, 2 * j:2 * j + 2].rearrange("p c n -> p (c n)"), ps[3 + j][:], ACT.Gelu)\
                        .then_inc(s_gelu, 1)
                if e + 1 < E:
                    evict_scatter(e + 1)

        @block.vector
        def _(dve):
            links = n_split = 0

            def link(ins):
                nonlocal links
                links += 1
                ins.then_inc(s_dve, 1)
                dve.wait_ge(s_dve, links)

            def statistics(n, b):
                for t in range(NT):
                    ins = dve.bn_stats(stats[:, t], x_sb[:, b, t])
                link(ins)
                for t in range(NT):
                    ins = dve.bn_aggr(mv[:, NT * b + t], stats[:, t])
                link(ins)
                dve.tensor_scalar(veps[:, NT * b:NT * b + NT], mv[:, NT * b:NT * b + NT, 1], EPS, None, ALU.add)\
                    .then_inc(s_var, 1)

            def normalise_tokens(n, b):
                dve.wait_ge(s_rstd, n + 1)
                for t in range(NT):
                    i = NT * b + t
                    ins = dve.tensor_scalar(xn[:, b, t], x_sb[:, b, t], mv[:, i, 0:1], rstd[:, i:i + 1],
                                            ALU.subtract, ALU.mult)
                ins.then_inc(s_xn, 1)

            def split(bank, width, bias, scale):
                nonlocal n_split
                p = parts[n_split % 2]
                if n_split >= 2:
                    dve.wait_ge(s_scr, 16 * PARTS * (n_split - 1))
                n_split += 1
                f, r = full[:, 0:width], rest[:, 0:width]
                link(dve.tensor_scalar(f, bank[:, 0:width], bias, scale, ALU.add, ALU.mult))
                link(dve.tensor_copy(p[:, 0, 0:width], f))
                link(dve.tensor_tensor(r, f, p[:, 0, 0:width], ALU.subtract))
                link(dve.tensor_copy(p[:, 1, 0:width], r))
                dve.tensor_tensor(p[:, 2, 0:width], r, p[:, 1, 0:width], ALU.subtract).then_inc(s_parts, 1)

            for b in range(B):
                dve.wait_ge(s_x[b], 16)
                statistics(b, b)
            dve.wait_ge(s_w, 16 * NW)
            link(dve.tensor_copy(identb[:], ident_sb[:]))
            for b in range(B):
                normalise_tokens(b, b)
            dve.wait_ge(s_proj, 1)
            split(ps[0], B * MP, bk_sb[:, 0:1], 1.0)
            for b in range(B):
                dve.wait_ge(s_proj, proj_qkv(b, 0))
                split(ps[(4, 7)[b]], S, 0.0, SCALE)
                dve.wait_ge(s_proj, proj_qkv(b, 1))
                split(ps[(5, 0)[b]], S, 0.0, 1.0)
            dve.wait_ge(s_v, B)
            for b in range(B):
                v = V2s[:, b, :, 0:HD]
                link(dve.tensor_tensor(v, v, bv_sb[:].rearrange("p (h d) -> p h d", d=HD), ALU.add))

            def maxima(n, half):
                units = max_units(groups[n][0])
                cut = (len(units) + 1) // 2
                seq = mx_first[n] + (cut if half else 0)
                for t, heads, keys in (units[cut:] if half else units[:cut]):
                    dve.wait_ge(s_mx, seq + 1)
                    bank = mx_banks[seq % MXB][:, 0:len(heads) * keys].rearrange("p (h k) -> p h k", k=keys)
                    ins = dve.tensor_reduce(nmax[:, t, heads[0]:heads[0] + len(heads)], bank, AX.X, ALU.max,
                                            negate=True)
                    ins.then_inc(s_mxfree, 1)
                    seq += 1
                if half:
                    dve.wait_ge(s_mxfree, mx_first[n + 1])

            def split_maxima(n):
                if n >= 2:
                    dve.wait_ge(s_nmTp, n - 1)
                link(dve.tensor_copy(nmp[n % 2][:, :, 0, :], nmax[:]))
                ins = dve.tensor_tensor(nmp[n % 2][:, :, 1, :], nmax[:], nmp[n % 2][:, :, 0, :], ALU.subtract)
                ins.then_inc(s_nmp, 1)
                dve.wait_ge(s_nmp, n + 1)

            def divide(n):
                kind, b, g = groups[n]
                dve.wait_ge(s_oTp, n + 1)
                tp = tp_bank[:].rearrange("p (t h w) -> p t h w", t=NT, w=VW)
                link(dve.reciprocal(rden[:], tp[:, :, :, HD]))
                w = G * HD
                o = on[b][:, :, w * g:w * g + w].rearrange("p t (h d) -> p t h d", d=HD)
                ins = dve.tensor_tensor(o, tp[:, :, :, 0:HD], rden[:].unsqueeze(3).to_broadcast([P, NT, G, HD]),
                                        ALU.mult)
                ins.then_inc(s_on, 1)
                dve.wait_ge(s_on, n + 1)

            def pipeline(n0, n1):
                for n in range(n0, n0 + LEAD):
                    maxima(n, 0)
                    maxima(n, 1)
                    split_maxima(n)
                for n in range(n0, n1):
                    if n + LEAD < n1:
                        maxima(n + LEAD, 0)
                        maxima(n + LEAD, 1)
                    if n > n0:
                        divide(n - 1)
                    if n + LEAD < n1:
                        split_maxima(n + LEAD)
                divide(n1 - 1)

            pipeline(0, B * NG)
            for b in range(B):
                dve.wait_ge(s_onTp, b + 1)
                dve.tensor_copy(onT[:, b], ps[4 * b][:]).then_inc(s_onT, 1)
            for b in range(B):
                dve.wait_ge(s_res, b + 1)
                xb = x_sb[:, b].rearrange("p t c -> p (t c)")
                link(dve.tensor_tensor(xb, ps[4 * b + 1][:], xb, ALU.add))
                statistics(B + b, b)
                normalise_tokens(B + b, b)
                dve.wait_ge(s_proj, proj_q2(b))
                split(ps[4 * b + 3], S, bq_sb[:, 0:1], SCALE)
            pipeline(B * NG, NGR)
            for b in range(B):
                dve.wait_ge(s_onTp, B + b + 1)
                dve.tensor_copy(onT[:, b], ps[4 * b][:]).then_inc(s_onT, 1)
                link(dve.tensor_tensor(x_sb[:, b], x_sb[:, b], b2_sb[:].unsqueeze(1).to_broadcast([P, NT, C]),
                                       ALU.add))
            for b in range(B):
                dve.wait_ge(s_res, B + b + 1)
                xb = x_sb[:, b].rearrange("p t c -> p (t c)")
                link(dve.tensor_tensor(xb, ps[4 * b + 3][:], xb, ALU.add))
                statistics(2 * B + b, b)
                normalise_tokens(2 * B + b, b)

            dve.wait_ge(s_gate, 1)
            z = ps[1][:, 0:NB8 * E].rearrange("p (n e) -> p n e", e=E)
            link(dve.tensor_reduce(gmax[:], z, AX.X, ALU.max))
            dve.tensor_tensor(pr[:], z, gmax[:].unsqueeze(2).to_broadcast([P, NB8, E]), ALU.subtract)\
                .then_inc(s_gz, 1)
            dve.wait_ge(s_gexp, 1)
            link(dve.tensor_reduce(gsum[:], pr[:], AX.X, ALU.add))
            link(dve.reciprocal(gmax[:], gsum[:]))
            dve.tensor_tensor(pr[:], pr[:], gmax[:].unsqueeze(2).to_broadcast([P, NB8, E]), ALU.mult)\
                .then_inc(s_pr, 1)
            dve.wait_ge(s_prT, 1)
            link(dve.tensor_copy(work[:], ps[2][0:B * E, :]))
            for r in range(CAP // 8):
                link(dve.max(top8[:], work[:]))
                link(dve.match_replace(work[:], top8[:], work[:], -1.0))
            link(dve.tensor_scalar(sel[:], work[:], 0.0, None, ALU.is_lt))
            link(dve.tensor_tensor_scan(slot[:], sel[:], ones[:], 0.0, ALU.add, ALU.mult))
            dve.tensor_tensor(slot[:], slot[:], sel[:], ALU.mult).then_inc(s_slot, 1)
            dve.wait_ge(s_slotT, 1)
            link(dve.tensor_copy(slT[:], ps[5][:, 0:NT * B * E].rearrange("p (t n) -> p t n", t=NT)))

            def choose(e):
                if e >= 2:
                    dve.wait_ge(s_gather, e - 1)
                for b in range(B):
                    for t in range(NT):
                        n = b * E + e
                        ins = dve.tensor_scalar(onehot[e % 2][:, b, t], iota_sb[:], slT[:, t, n:n + 1], None,
                                                ALU.is_equal)
                ins.then_inc(s_onehot, 1)
                if e >= 2:
                    dve.wait_ge(s_scp, e - 1)
                for b in range(B):
                    for t in range(NT):
                        n = b * E + e
                        ins = dve.tensor_scalar(weighted[e % 2][:, b, t], iota_sb[:], slT[:, t, n:n + 1],
                                                pr[:, t * B + b, e:e + 1], ALU.is_equal, ALU.mult)
                ins.then_inc(s_weighted, 1)

            def evict_gather(e):
                dve.wait_ge(s_gather, e + 1)
                if e >= 1:
                    dve.wait_ge(s_hid, e)
                dve.tensor_copy(xin, ps[2][:, 0:B * CAP]).then_inc(s_xin, 1)

            choose(0)
            choose(1)
            evict_gather(0)
            for e in range(E):
                if e + 1 < E:
                    evict_gather(e + 1)
                dve.wait_ge(s_yp, e + 1)
                if e >= 1:
                    dve.wait_ge(s_comb, e)
                dve.tensor_copy(y_sb, ps[5][:, 0:B * C].rearrange("p (b c) -> p b c", b=B)).then_inc(s_y, 1)
                if e + 2 < E:
                    choose(e + 2)
            dve.wait_ge(s_comb, E)
            for b in range(B):
                xb = x_sb[:, b].rearrange("p t c -> p (t c)")
                dve.tensor_tensor(xb, ps[b][:], xb, ALU.add).then_inc(s_fin, 1)

        @block.tensor
        def _(pe):
            def transposed(bank, src, b, n):
                for t in range(NT):
                    ins = pe.transpose(bank[:, t * P:(t + 1) * P], src[:, b, t] if n else src[:, t], ident_sb[:])
                return ins

            pe.wait_ge(s_w, 16 * NW)
            pe.matmul(ps[0][:, 0:B * MP], wk_sb[:], ctxT_sb[:].rearrange("p b m -> p (b m)"), start=True, stop=True)\
                .then_inc(s_proj, 1)
            for b in range(B):
                ins = pe.matmul(ps[1][0:M, b * C:(b + 1) * C], ctxT_sb[:, b, 0:M], wv_sb[:], start=True, stop=True)
            ins.then_inc(s_proj, 1)
            for b in range(B):
                pe.wait_ge(s_xn, b + 1)
                transposed(ps[2 + b], xn, b, 1).then_inc(s_xnTp, 1)
            for b in range(B):
                pe.wait_ge(s_xnT, b + 1)
                pe.matmul(ps[(4, 7)[b]][:], wqkvT_sb[:, 0:C], xnT[:, b], start=True, stop=True).then_inc(s_proj, 1)
                if b:
                    pe.wait_ge(s_parts, 1)
                pe.matmul(ps[(5, 0)[b]][:], wqkvT_sb[:, C:2 * C], xnT[:, b], start=True, stop=True)\
                    .then_inc(s_proj, 1)
                if b:
                    pe.wait_ge(s_v, B)
                for t in range(NT):
                    ins = pe.matmul(ps[(6, 1)[b]][:, t * C:(t + 1) * C], xnT[:, b, t * P:(t + 1) * P],
                                    wqkvT_sb[:, 2 * C:3 * C], start=True, stop=True)
                ins.then_inc(s_proj, 1)

            def operands(kind, b):
                if kind == "self":
                    return Qs[b], Ks[b]
                return Qs[b], K2s[:, :, b, :]

            def max_scores(n, half):
                kind, b, g = groups[n]
                q, k = operands(kind, b)
                units = max_units(kind)
                cut = (len(units) + 1) // 2
                seq = mx_first[n] + (cut if half else 0)
                if not half:
                    pe.wait_ge(s_stack[n], 16 * (12 if kind == "self" else 9))
                for t, heads, keys in (units[cut:] if half else units[:cut]):
                    if seq >= MXB:
                        pe.wait_ge(s_mxfree, seq - MXB + 1)
                    bank = mx_banks[seq % MXB]
                    for i, h in enumerate(heads):
                        diag = kind == "self"
                        ins = pe.matmul(bank[:, i * keys:(i + 1) * keys],
                                        q[0:MAXROW, G * g + h, t * P:(t + 1) * P],
                                        k[0:MAXROW, G * g + h, 0:keys], start=(i == 0), stop=not diag,
                                        skip_group_check=True)
                        if diag:
                            ins = pe.matmul(bank[:, (i + 1) * keys - P:(i + 1) * keys], identb[:], maskb[:],
                                            start=False, stop=True, skip_group_check=True)
                    ins.then_inc(s_mx, 1)
                    seq += 1

            def scores(n, p):
                kind, b, g = groups[n]
                q, k = operands(kind, b)
                units = exp_units(kind)
                seq = st_first[n] + sum(len(u) for u in units[:p])
                if p == 0:
                    pe.wait_ge(s_nmrow[n % 2], 32 * (n // 2 + 1))
                for at, width, blocks in units[p]:
                    if seq >= STB:
                        pe.wait_ge(s_exp, seq - STB + 1)
                    for i, (h, j, col, qt) in enumerate(blocks):
                        if kind == "self":
                            rows, keys = P, k[:, G * g + h, j * P:(j + 1) * P]
                        else:
                            rows, keys = M, k[:, G * g + h, 0:M]
                        ins = pe.matmul(st_banks[seq % STB][0:rows, col:col + S - qt * P], keys,
                                        q[:, G * g + h, qt * P:S], start=(i == 0), stop=True, skip_group_check=True)
                    ins.then_inc(s_st, 1)
                    seq += 1

            def values(n):
                kind, b, g = groups[n]
                if kind == "self":
                    pe.wait_ge(s_causal, st_first[n + 1])
                else:
                    pe.wait_ge(s_exp, st_first[n + 1])
                if n > 0:
                    pe.wait_ge(s_oT, n)
                blocks = [(j, h, at + col, qt) for units in exp_units(kind) for at, _, bl in units
                          for h, j, col, qt in bl]
                last = NT - 1 if kind == "self" else 0
                for j, h, at, qt in sorted(blocks):
                    if kind == "self":
                        v, rows = Vs[b][:, j, G * g + h, :], P
                    else:
                        v, rows = V2s[:, b, G * g + h, :], M
                    ins = pe.matmul(pv_bank[VW * h:VW * h + VW, qt * P:S], v,
                                    prob[n % 2][0:rows, at:at + S - qt * P], start=(j == 0), stop=(j == last),
                                    tile_position=(0, VW * h), skip_group_check=True)
                ins.then_inc(s_pv, 1)

            def transpose_maxima(n, free):
                free()
                pe.wait_ge(s_nmp, n + 1)
                for t in range(NT):
                    ins = pe.transpose(tp_bank[:].bitcast(BF16)[0:2 * G, t * P:(t + 1) * P],
                                       nmp[n % 2][:, t].rearrange("p i h -> p (i h)"), identb[:])
                ins.then_inc(s_nmTp, 1)

            def transpose_outputs(n, free):
                free()
                pe.wait_ge(s_oT, n + 1)
                for t in range(NT):
                    ins = pe.transpose(tp_bank[:, t * P:(t + 1) * P], oT[:, t * P:(t + 1) * P], ident_sb[:])
                ins.then_inc(s_oTp, 1)

            def pipeline(n0, n1):
                maxima_copied = lambda n: (lambda: pe.wait_ge(s_nmT, n + 1))
                outputs_divided = lambda n: (lambda: pe.wait_ge(s_on, n + 1))
                free = lambda: None
                for n in range(n0, n0 + LEAD):
                    max_scores(n, 0)
                    max_scores(n, 1)
                    transpose_maxima(n, free)
                    free = maxima_copied(n)
                for n in range(n0, n1):
                    scores(n, 0)
                    if n + LEAD < n1:
                        max_scores(n + LEAD, 0)
                    if n > n0:
                        values(n - 1)
                    scores(n, 1)
                    if n + LEAD < n1:
                        max_scores(n + LEAD, 1)
                    if n > n0:
                        transpose_outputs(n - 1, free)
                        free = outputs_divided(n - 1)
                    if n + LEAD < n1:
                        transpose_maxima(n + LEAD, free)
                        free = maxima_copied(n + LEAD)
                values(n1 - 1)
                transpose_outputs(n1 - 1, free)

            pe.wait_ge(s_const, 5)
            pe.wait_ge(s_rows, 16 * (3 * B + 1))
            pe.wait_ge(s_xnT, B)
            pe.wait_ge(s_v, 2 * B)
            pe.wait_ge(s_parts, 1 + 2 * B)
            pipeline(0, B * NG)
            for b in range(B):
                pe.wait_ge(s_on, B * NG)
                transposed(ps[4 * b], on[b], b, 0).then_inc(s_onTp, 1)
            for b in range(B):
                pe.wait_ge(s_onT, b + 1)
                for t in range(NT):
                    ins = pe.matmul(ps[4 * b + 1][:, t * C:(t + 1) * C], onT[:, b, t * P:(t + 1) * P], woT_sb[:],
                                    start=True, stop=True)
                ins.then_inc(s_res, 1)
            for b in range(B):
                pe.wait_ge(s_xn, B + b + 1)
                transposed(ps[2 + 4 * b], xn, b, 1).then_inc(s_xnTp, 1)
                pe.wait_ge(s_xnT, B + b + 1)
                pe.matmul(ps[3 + 4 * b][:], wq_sb[:], xnT[:, b], start=True, stop=True).then_inc(s_proj, 1)
            pe.wait_ge(s_parts, 1 + 3 * B)
            pe.wait_ge(s_k2, 16 * PARTS)
            pipeline(B * NG, NGR)
            for b in range(B):
                pe.wait_ge(s_on, NGR)
                transposed(ps[4 * b], on[b], b, 0).then_inc(s_onTp, 1)
            for b in range(B):
                pe.wait_ge(s_onT, B + b + 1)
                for j in range(2):
                    ins = pe.matmul(ps[4 * b + 1 + j][:], w1_sb[:, j * C:(j + 1) * C], onT[:, b], start=True,
                                    stop=True)
                ins.then_inc(s_h1p, 1)
            for b in range(B):
                pe.wait_ge(s_h1, 2 * b + 2)
                for t in range(NT):
                    for j in range(2):
                        ins = pe.matmul(ps[4 * b + 3][:, t * C:(t + 1) * C], h1[:, b, j, t * P:(t + 1) * P],
                                        w2_sb[:, j], start=(j == 0), stop=(j == 1), skip_group_check=True)
                ins.then_inc(s_res, 1)
            for b in range(B):
                pe.wait_ge(s_xn, 2 * B + b + 1)
                transposed(ps[4 * b], xn, b, 1).then_inc(s_xnTp, 1)

            pe.wait_ge(s_xnT, 3 * B)
            for t in range(NT):
                for b in range(B):
                    i = (t * B + b) * E
                    ins = pe.matmul(ps[1][:, i:i + E], xnT[:, b, t * P:(t + 1) * P], gw_sb[:], start=True, stop=True)
            ins.then_inc(s_gate, 1)
            pe.wait_ge(s_pr, 1)
            for t in range(NT):
                ins = pe.transpose(ps[2][0:B * E, t * P:(t + 1) * P],
                                   pr[:, t * B:(t + 1) * B].rearrange("p b e -> p (b e)"), ident_sb[:])
            ins.then_inc(s_prT, 1)
            pe.wait_ge(s_slot, 1)
            for t in range(NT):
                n = B * E
                ins = pe.transpose(ps[5][:, t * n:(t + 1) * n], slot[:, t * P:(t + 1) * P], ident_sb[0:n, 0:n])
            ins.then_inc(s_slotT, 1)

            def gather(e):
                pe.wait_ge(s_onehot, e + 1)
                if e >= 1:
                    pe.wait_ge(s_xin, e)
                for b in range(B):
                    for t in range(NT):
                        ins = pe.matmul(ps[2][:, b * CAP:(b + 1) * CAP], xn[:, b, t], onehot[e % 2][:, b, t],
                                        start=(t == 0), stop=(t == NT - 1), skip_group_check=True)
                ins.then_inc(s_gather, 1)

            def turn_weights(e):
                pe.wait_ge(s_weighted, e + 1)
                if e >= 1:
                    pe.wait_ge(s_sc, 2 * e)
                for b in range(B):
                    for t in range(NT):
                        ins = pe.transpose(ps[6 + b][:, t * P:(t + 1) * P], weighted[e % 2][:, b, t], ident_sb[:])
                ins.then_inc(s_scp, 1)

            gather(0)
            turn_weights(0)
            pe.wait_ge(s_moew, 32)
            for e in range(E):
                pe.wait_ge(s_xin, e + 1)
                if e >= 1:
                    pe.wait_ge(s_gelu, 2 * e)
                for c in range(NC):
                    ins = pe.matmul(ps[3 + c // 2][:, (c % 2) * B * CAP:(c % 2 + 1) * B * CAP],
                                    mw1_sb[:, e, c * P:(c + 1) * P], xin, start=(c % 2 == 0), stop=True,
                                    skip_group_check=True)
                ins.then_inc(s_hid, 1)
                if e + 1 < E:
                    gather(e + 1)
                pe.wait_ge(s_gelu, 2 * e + 2)
                if e >= 1:
                    pe.wait_ge(s_y, e)
                for b in range(B):
                    for c in range(NC):
                        ins = pe.matmul(ps[5][:, b * C:(b + 1) * C], hidden[:, c, b * CAP:(b + 1) * CAP],
                                        mw2_sb[:, e, c], start=(c == 0), stop=(c == NC - 1), skip_group_check=True)
                ins.then_inc(s_yp, 1)
                if e + 1 < E:
                    turn_weights(e + 1)
                pe.wait_ge(s_y, e + 1)
                pe.wait_ge(s_sc, 2 * e + 2)
                for b in range(B):
                    for t in range(NT):
                        ins = pe.matmul(ps[b][:, t * C:(t + 1) * C], scatter[e % 2][:, b, t], y_sb[:, b],
                                        start=(e == 0 and t == 0), stop=(e == E - 1), skip_group_check=True)
                ins.then_inc(s_comb, 1)



def bf16_parts(v):
    out = []
    for _ in range(PARTS):
        hi = (v.view(np.uint32) & np.uint32(0xFFFF0000)).view(np.float32)
        out.append((hi.view(np.uint32) >> 16).astype(np.uint16))
        v = (v - hi).astype(np.float32)
    return np.stack(out)


def shape_constants():
    slopes = np.float32([(2.0 ** -0.5) ** (i + 1) for i in range(H)])
    alibi = -(slopes[:, None] * np.arange(S, dtype=np.float32)[None, :])
    one = np.uint16(0x3F80)
    return {
        "alibi": bf16_parts(np.ascontiguousarray(alibi)),
        "ones_rows": np.full((3, H, S), one, np.uint16),
        "ident": np.eye(P, dtype=np.float32),
        "iota1": np.ascontiguousarray(np.broadcast_to(np.arange(1, P + 1, dtype=np.float32), (P, P))),
    }


def kernel(x, ctx_768, L0_attn_W_qkv, L0_attn_W_o, L0_xattn_Wq, L0_xattn_bq, L0_xattn_Wk, L0_xattn_bk,
           L0_xattn_Wv, L0_xattn_bv, L0_xattn_W1, L0_xattn_b1, L0_xattn_W2, L0_xattn_b2, L0_ffn_gate_w,
           L0_ffn_w1, L0_ffn_w2):
    import concourse.bacc as bacc
    from concourse.bass_utils import run_bass_kernel_spmd

    a = np.asarray
    data = {
        "x": a(x),
        "ctxT": a(ctx_768).transpose(2, 0, 1),
        "wqkvT": a(L0_attn_W_qkv).T,
        "woT": a(L0_attn_W_o).T,
        "wq": a(L0_xattn_Wq), "bq": a(L0_xattn_bq).reshape(C, 1),
        "wk": a(L0_xattn_Wk), "bk": a(L0_xattn_bk).reshape(C, 1),
        "wv": a(L0_xattn_Wv), "bv": a(L0_xattn_bv),
        "w1": a(L0_xattn_W1), "b1": a(L0_xattn_b1).reshape(2, C).T,
        "w2": a(L0_xattn_W2).reshape(2, C, C).transpose(1, 0, 2), "b2": a(L0_xattn_b2),
        "gate_w": a(L0_ffn_gate_w),
        "mw1": a(L0_ffn_w1).transpose(1, 0, 2),
        "mw2": a(L0_ffn_w2).reshape(E, NC, P, C).transpose(2, 0, 1, 3),
        **shape_constants(),
    }
    nc = bacc.Bacc("TRN2", target_bir_lowering=False, num_devices=1)
    arrays, args = {}, {}
    for name, v in data.items():
        v = np.ascontiguousarray(v)
        arrays[f"in_{name}"] = v
        t = nc.dram_tensor(f"in_{name}", v.shape, mybir.dt.from_np(v.dtype), kind="ExternalInput").ap()
        args[name] = t.bitcast(BF16) if v.dtype == np.uint16 else t
    out = nc.dram_tensor("out", (B, S, C), F32, kind="ExternalOutput").ap()
    decoder_block(nc, out=out, **args)
    r = run_bass_kernel_spmd(nc, [arrays], core_ids=[0])
    return r.results[0]["out"]
```

```python
from contextlib import ExitStack

import numpy as np

import concourse.bass as bass
from concourse import mybir

F32 = mybir.dt.float32
BF16 = mybir.dt.bfloat16
F32R = mybir.dt.float32r
ALU = mybir.AluOpType
ACT = mybir.ActivationFunctionType
AX = mybir.AxisListType

P = 128
B, S, C, H = 2, 512, 128, 16
HD = C // H
NT = S // P
M, CT = 77, 96
MP = 80
E, CAP, FF = 8, 2 * S // 8, 512
NC = FF // P
G = 4
NG = H // G
SCALE = float(np.float32(HD ** -0.5))
EPS = 1e-5

PARTS = 3
SLOT_ROWS = PARTS * PARTS * HD
ALIBI = SLOT_ROWS
MAXROW = 96
ROWS = MAXROW + 2
VW = 32


def max_units(kind):
    if kind == "cross":
        return [(t, tuple(range(G)), M) for t in range(NT)]
    return ([(3, (h,), 4 * P) for h in range(G)] + [(2, (h,), 3 * P) for h in range(G)]
            + [(1, (0, 1), 2 * P), (1, (2, 3), 2 * P), (0, (0, 1, 2, 3), P)])


def exp_units(kind):
    if kind == "cross":
        return [(S * h, S, [(h, 0, 0, 0)]) for h in range(G)]
    units = []
    for a in (0, 2):
        for h in (a, a + 1):
            units.append((2 * S * h, S, [(h, 0, 0, 0)]))
            units.append((2 * S * h + S, S, [(h, 1, 0, 1), (h, 3, 3 * P, 3)]))
        units.append((2 * S * G + S * (a // 2), S, [(a, 2, 0, 2), (a + 1, 2, 2 * P, 2)]))
    return units


def together(*streams):
    clocks, places, merged = [0.0] * len(streams), [0] * len(streams), []
    while any(p < len(st) for p, st in zip(places, streams)):
        _, i = min((c, i) for i, c in enumerate(clocks) if places[i] < len(streams[i]))
        weight, entry = streams[i][places[i]]
        merged.append((weight, entry))
        clocks[i] += weight
        places[i] += 1
    return merged


def schedule():
    def maxima(n):
        return [(0.6, ("max", n, i)) for i in range(len(max_units(KIND(n))))] + [(1.0, ("negmax", n)), (0, ("negrow", n))]

    def finish(n):
        return [(0.9, ("values", n, j)) for j in range(NT if KIND(n) == "self" else 1)] \
            + [(0.6, ("values_out", n)), (1.2, ("output", n))]

    def step(n, ahead=()):
        entries = []
        add = entries.append
        exp = [("scores", n, i) for i in range(len(exp_units(KIND(n))))]
        mx = [("max", m, i) for m in ahead for i in range(len(max_units(KIND(m))))]
        n_slots = max(len(exp), len(mx))
        chunks = [entry for _, entry in finish(n - 1)] if n not in FIRST else []
        for i in range(n_slots):
            if i < len(exp):
                add((W_SLOT, exp[i]))
            for _ in range(-(-len(mx) // (n_slots - i))):
                add((0 if i < len(exp) else W_SLOT, mx.pop(0)))
                m, last = entries[-1][1][1:]
                if last == len(max_units(KIND(m))) - 1:
                    add((0, ("negmax", m)))
                    pending.append((m, i))
            if pending and (pending[0][1] + 2 == i or pending[0][1] > i >= 1):
                add((0, ("negrow", pending.pop(0)[0])))
            if chunks and i >= (3 if n_slots > 6 else 1):
                add((0, chunks.pop(0)))
        entries.extend((W_SLOT / 2, c) for c in chunks)
        return entries

    pending = []
    W_SLOT = 0.85

    def tail(b):
        return [(1.6, ("onT", b)), (2.4, ("residual", b)), (2.0, ("norm", b)), (1.8, ("xnT", 1, b)), (4, ("q2", b))]

    def mlp(b):
        return [(1.6, ("onT", B + b)), (1.8, ("hidden", b, 0)), (1.8, ("hidden", b, 1)), (3.4, ("mlp", b)),
                (2.0, ("norm", B + b)), (1.8, ("xnT", 2, b)), (2.2, ("gate", b)), (1.2, ("probs", b)),
                (1.5, ("choice", b))]

    def selection(b):
        return [(1.4, ("top", b, r)) for r in range(ROUNDS)] + [(1.6, ("slots", b)), (1, ("slotsT", b))]

    def experts(b):
        first, last = b * E, (b + 1) * E
        entries = [("choose", first), ("gather", first), ("turn", first), ("choose", first + 1)]
        for k in range(first, last):
            entries.append(("experts_hidden", k))
            if k + 1 < last:
                entries.append(("gather", k + 1))
            if k + 2 < last:
                entries.append(("choose", k + 2))
            entries.append(("experts_out", k))
            if k > first:
                entries.append(("combine", k - 1))
            if k + 1 < last:
                entries.append(("turn", k + 1))
        entries += [("combine", last - 1), ("combined", b)]
        return [(W_EXPERT / 6, entry) for entry in entries]

    W_EXPERT = 3.5
    order = maxima(0) + maxima(1) + [(0, ("context_keys",))]
    order += step(0, [2]) + step(1, [3]) + step(2, [4]) + step(3, [5]) + step(4, [6])
    order += together(step(5, [7]) + step(6) + step(7, [8, 9]), tail(0))
    order += step(8, [10])
    order += together(step(9, [11]) + step(10) + step(11) + finish(11), tail(1))
    order += together(maxima(12) + maxima(13) + step(12, [14]) + step(13, [15]) + step(14) + step(15) + finish(15)
                      + mlp(1), mlp(0) + selection(0), [(5, ("weights", i)) for i in range(4)])
    order += together(experts(0), selection(1))
    order += together(experts(1), [(1, None), (1, ("finish", 0))])
    order.append((0, ("finish", 1)))
    return [entry for _, entry in order if entry]


GROUPS = [("self", b, g) for b in range(B) for g in range(NG)] + [("cross", b, g) for b in range(B) for g in range(NG)]
NGR = len(GROUPS)
ROUNDS = CAP // 8
FIRST = (0, 12)


def KIND(n):
    return GROUPS[n][0]


MX_FIRST, ST_FIRST = [0], [0]
for _kind, _, _ in GROUPS:
    MX_FIRST.append(MX_FIRST[-1] + len(max_units(_kind)))
    ST_FIRST.append(ST_FIRST[-1] + len(exp_units(_kind)))


def play(handlers):
    for what, *args in schedule():
        if what in handlers:
            handlers[what](*args)


def split(engine, link, parts, value, rest):
    link(engine.tensor_copy(parts[:, 0], value))
    link(engine.tensor_tensor(rest, value, parts[:, 0], ALU.subtract))
    link(engine.tensor_copy(parts[:, 1], rest))
    return engine.tensor_tensor(parts[:, 2], rest, parts[:, 1], ALU.subtract)


def decoder_block(nc, x, first, ctxw, late, rows, k_fixed, q_fixed, k2_fixed, mw1, mw2, out):
    MXB, STB = 3, 3
    ctx = ExitStack()
    with ctx:
        def sb(name, shape, dt=F32):
            return ctx.enter_context(nc.sbuf_tensor(name, shape, dt))

        def sem(name):
            return ctx.enter_context(nc.semaphore(name))

        def cut(tile, *widths):
            at, res = 0, []
            for w in widths:
                res.append(tile[:, at:at + w])
                at += w
            return res

        ps = [ctx.enter_context(nc.psum_tensor(f"bank{i}", [P, 512], F32)) for i in range(8)]
        mx_banks = [ps[2], ps[3], ps[6]]
        st_banks = [ps[4], ps[5], ps[7]]
        pv_bank, tp_bank = ps[0], ps[1]
        gather_banks, hid_banks, turn_bank, y_bank, comb_bank = [ps[2], ps[3]], [ps[5], ps[6]], ps[4], ps[7], ps[0]

        x_sb = sb("x_sb", [P, B, NT, C])
        xn = sb("xn", [P, B, NT, C])
        xnT = sb("xnT", [P, B, S])
        stats = sb("stats", [P, NT, 6])
        mv = sb("mv", [P, B * NT, 2])
        veps = sb("veps", [P, B * NT])
        rstd = sb("rstd", [P, B * NT])
        neghalf = sb("neghalf", [P, NT])
        first_sb = sb("first_sb", [P, 4 * C])
        wqkvT_sb, ident_sb = cut(first_sb, 3 * C, C)
        ctxw_sb = sb("ctxw_sb", [CT, 2 * C + B * MP])
        wk_sb, wv_sb, ctxT_sb = cut(ctxw_sb, C, C, B * MP)
        late_sb = sb("late_sb", [P, 7 * C + 4 + E])
        woT_sb, wq_sb, w1_sb, w2_sb, iota_sb, b1_sb, bq_sb, bk_sb, gw_sb = cut(late_sb, C, C, 2 * C, 2 * C, C, 2, 1, 1, E)
        rows_sb = sb("rows_sb", [P, 2 * C])
        bv_sb, b2_sb = rows_sb[0:M, 0:C], rows_sb[:, C:2 * C]
        identb = sb("identb", [P, P], BF16)
        maskb = sb("maskb", [P, P], BF16)
        full = [sb(f"full{i}", [P, S]) for i in range(3)]
        rest = [sb(f"rest{i}", [P, S]) for i in range(3)]
        qparts = [sb(f"qparts{i}", [P, PARTS, S], BF16) for i in range(2)]
        kparts = [sb(f"kparts{i}", [P, PARTS, S], BF16) for i in range(2)]
        Qs = [sb(f"Qs{b}", [P, H, S], BF16) for b in range(B)]
        Ks = [sb(f"Ks{b}", [P, H, S], BF16) for b in range(B)]
        K2s = sb("K2s", [P, H, B * MP], BF16)
        Vs = [sb(f"Vs{b}", [P, NT, H, VW]) for b in range(B)]
        V2s = sb("V2s", [M, B, H, VW])
        prob = [sb(f"prob{i}", [P, 5 * 2 * S]) for i in range(2)]
        nmax = [sb(f"nmax{i}", [P, NT, G]) for i in range(2)]
        nmp = [sb(f"nmp{i}", [P, NT, 2, G], BF16) for i in range(2)]
        nmT = [sb(f"nmT{i}", [2 * G, S], BF16) for i in range(2)]
        oT = [sb(f"oT{i}", [P, S]) for i in range(2)]
        rden = sb("rden", [P, NT, G])
        on = [sb(f"on{b}", [P, NT, C]) for b in range(B)]
        onT = sb("onT", [P, S])
        mw1_sb = Ks[0][:].rearrange("p h s -> p (h s)").bitcast(F32).rearrange("p (e f) -> p e f", e=E)
        mw2_sb = Ks[1][:].rearrange("p h s -> p (h s)").bitcast(F32).rearrange("p (e c n) -> p e c n", e=E, c=NC)
        q32 = [Qs[b][:].rearrange("p h s -> p (h s)").bitcast(F32) for b in range(B)]
        h1 = [q32[b][:, 0:2 * S].rearrange("p (j s) -> p j s", j=2) for b in range(B)]
        work, sel, slot = ([q32[b][0:E, i * S:(i + 1) * S] for b in range(B)] for i in (2, 3, 4))
        ones = sb("ones", [E, S])
        top8 = sb("top8", [E, 8])
        gmax = sb("gmax", [P, NT])
        gsum = sb("gsum", [P, NT])
        pr = [sb(f"pr{b}", [P, NT, E]) for b in range(B)]
        pr_rest = sb("pr_rest", [P, NT, E])
        prs = [sb(f"prs{b}", [P, PARTS, NT, E], BF16) for b in range(B)]
        xns = [sb(f"xns{b}", [P, PARTS, NT, C], BF16) for b in range(B)]
        onehot = [sb(f"onehot{i}", [P, NT, CAP], BF16) for i in range(2)]
        scatter = [sb(f"scatter{i}", [P, S], F32R) for i in range(2)]
        ys = [sb(f"ys{i}", [P, 2, C], F32R) for i in range(2)]
        slT = [sb(f"slT{b}", [P, NT, E]) for b in range(B)]
        pslot = [sb(f"pslot{i}", [P, 1]) for i in range(2)]
        combT = [oT[b] for b in range(B)]
        hidden = [prob[0][:, i * S:(i + 1) * S] for i in range(2)]
        xin = [prob[1][:, i * CAP:(i + 1) * CAP] for i in range(2)]

        q_scr = [nc.dram_tensor(f"q_scr{i}", (PARTS, HD * H, S), BF16, kind="Internal").ap() for i in range(2 * B)]
        k_scr = [nc.dram_tensor(f"k_scr{b}", (PARTS, HD * H, S), BF16, kind="Internal").ap() for b in range(B)]
        k2_scr = nc.dram_tensor("k2_scr", (PARTS, HD * H, B * MP), BF16, kind="Internal").ap()

        s_x = [sem(f"s_x{b}") for b in range(B)]
        s_first = sem("s_first")
        s_ctxw = sem("s_ctxw")
        s_late = sem("s_late")
        s_moew = sem("s_moew")
        s_const = sem("s_const")
        s_fixed = [sem(f"s_fixed{b}") for b in range(B)]
        s_fixed2 = sem("s_fixed2")
        s_vpad = sem("s_vpad")
        s_dve = sem("s_dve")
        s_pool = sem("s_pool")
        s_identb = sem("s_identb")
        s_var = sem("s_var")
        s_rstd = sem("s_rstd")
        s_xn = sem("s_xn")
        s_xnTp = sem("s_xnTp")
        s_xnT = sem("s_xnT")
        s_qp = sem("s_qp")
        s_kp = sem("s_kp")
        s_vp = sem("s_vp")
        s_qfull = sem("s_qfull")
        s_kfull = sem("s_kfull")
        s_qparts = sem("s_qparts")
        s_kparts = [sem(f"s_kparts{i}") for i in range(B + 1)]
        s_qscr = sem("s_qscr")
        s_kscr = sem("s_kscr")
        s_qstack = [sem(f"s_qstack{i}") for i in range(2 * B)]
        s_kstack = [sem(f"s_kstack{i}") for i in range(B + 1)]
        s_v = sem("s_v")
        s_v2 = sem("s_v2")
        s_mx = sem("s_mx")
        s_mxfree = sem("s_mxfree")
        s_nmp = sem("s_nmp")
        s_nmTp = sem("s_nmTp")
        s_nmT = sem("s_nmT")
        s_nmrow = [sem(f"s_nmrow{i}") for i in range(2)]
        s_st = sem("s_st")
        s_exp = sem("s_exp")
        s_causal = sem("s_causal")
        s_pv = sem("s_pv")
        s_oT = sem("s_oT")
        s_oTp = sem("s_oTp")
        s_on = sem("s_on")
        s_onTp = sem("s_onTp")
        s_onT = sem("s_onT")
        s_resp = sem("s_resp")
        s_res = sem("s_res")
        s_h1p = sem("s_h1p")
        s_h1 = sem("s_h1")
        s_xns = sem("s_xns")
        s_gate = sem("s_gate")
        s_gz = sem("s_gz")
        s_gexp = sem("s_gexp")
        s_pr = sem("s_pr")
        s_prs = sem("s_prs")
        s_prT = sem("s_prT")
        s_work = sem("s_work")
        s_slot = sem("s_slot")
        s_slotT = sem("s_slotT")
        s_slT = sem("s_slT")
        s_onehot = sem("s_onehot")
        s_gather = sem("s_gather")
        s_xin = sem("s_xin")
        s_pslot = sem("s_pslot")
        s_turn = sem("s_turn")
        s_scatter = sem("s_scatter")
        s_hid = sem("s_hid")
        s_gelu = sem("s_gelu")
        s_yp = sem("s_yp")
        s_yhi = sem("s_yhi")
        s_y = sem("s_y")
        s_comb = sem("s_comb")
        s_combT = sem("s_combT")
        s_combTp = sem("s_combTp")
        s_fin = sem("s_fin")
        s_out = sem("s_out")

        q_banks, k_banks, v_banks = (ps[4], ps[7]), (ps[5], ps[0], ps[5]), (ps[6], ps[1], ps[6])

        block = ctx.enter_context(nc.Block())

        @block.sync
        def _(sp):
            def stack_q(i, b):
                sp.wait_ge(s_qparts, i + 1)
                sp.dma_start(q_scr[i].rearrange("p c s -> c p s"), qparts[i % 2][:]).then_inc(s_qscr, 16)
                sp.wait_ge(s_qscr, 16 * (i + 1))
                rows = PARTS * HD
                if i >= B:
                    sp.wait_ge(s_st, ST_FIRST[NG * (b + 1)])
                for p in range(PARTS):
                    src = q_scr[i][p].rearrange("(d h) s -> d (h s)", d=HD).unsqueeze(0).to_broadcast([PARTS, HD, H * S])
                    sp.dma_start(Qs[b][rows * p:rows * p + rows].rearrange("p h s -> p (h s)"), src)\
                        .then_inc(s_qstack[i], 16)

            def stack_k(i, tile, scr, buf, width):
                sp.wait_ge(s_kparts[i], 1)
                sp.dma_start(scr.rearrange("p c s -> c p s"), buf[:, :, 0:width]).then_inc(s_kscr, 16)
                sp.wait_ge(s_kscr, 16 * (i + 1))
                rows = PARTS * HD
                src = scr.rearrange("p (d h) s -> (p d) (h s)", d=HD)
                for r in range(PARTS):
                    sp.dma_start(tile[rows * r:rows * r + rows].rearrange("p h s -> p (h s)"), src)\
                        .then_inc(s_kstack[i], 16)

            xv = x.rearrange("b (t p) c -> p b t c", p=P)
            sp.dma_start(x_sb[:, 0], xv[:, 0]).then_inc(s_x[0], 16)
            sp.dma_start(first_sb[:], first).then_inc(s_first, 16)
            sp.dma_start(x_sb[:, 1], xv[:, 1]).then_inc(s_x[1], 16)
            sp.dma_start(ctxw_sb[:], ctxw).then_inc(s_ctxw, 16)
            sp.dma_start(Ks[0][SLOT_ROWS:ROWS], k_fixed).then_inc(s_fixed[0], 16)
            sp.dma_start(Qs[0][SLOT_ROWS:ROWS], q_fixed).then_inc(s_fixed[0], 16)
            sp.dma_start(late_sb[:], late).then_inc(s_late, 16)
            sp.dma_start(rows_sb[:], rows.partition_broadcast(P)).then_inc(s_late, 16)
            stack_k(0, Ks[0], k_scr[0], kparts[0], S)
            stack_q(0, 0)
            sp.dma_start(Ks[1][SLOT_ROWS:ROWS], k_fixed).then_inc(s_fixed[1], 16)
            sp.dma_start(Qs[1][SLOT_ROWS:ROWS], q_fixed).then_inc(s_fixed[1], 16)
            stack_q(1, 1)
            stack_k(1, Ks[1], k_scr[1], kparts[1], S)

            def negmax(n):
                kind, b, g = GROUPS[n]
                sp.wait_ge(s_nmT, n + 1)
                sp.dma_start(Qs[b][MAXROW:ROWS, G * g:G * g + G], nmT[n % 2][:]).then_inc(s_nmrow[n % 2], 16)

            def context_keys():
                sp.dma_start(K2s[SLOT_ROWS:ROWS], k2_fixed).then_inc(s_fixed2, 16)
                stack_k(2, K2s, k2_scr, kparts[0], B * MP)

            def weights(i):
                if i == 0:
                    sp.wait_ge(s_st, ST_FIRST[B * NG])
                tile, src = ((mw1_sb, mw1), (mw2_sb, mw2))[i // 2]
                half = slice(i % 2 * (E // 2), (i % 2 + 1) * (E // 2))
                sp.dma_start(tile[:, half], src[:, half]).then_inc(s_moew, 16)

            def finish(b):
                sp.wait_ge(s_fin, b + 1)
                sp.dma_start(out.rearrange("b (t p) c -> p b t c", p=P)[:, b], x_sb[:, b]).then_inc(s_out, 16)

            play({"negrow": negmax, "q2": lambda b: stack_q(B + b, b), "finish": finish,
                  "context_keys": context_keys, "weights": weights})
            sp.wait_ge(s_out, 16 * B)

        @block.gpsimd
        def _(pool):
            links = 0

            def link(ins):
                nonlocal links
                links += 1
                ins.then_inc(s_pool, 1)
                pool.wait_ge(s_pool, links)

            def rstd_of(n, b):
                pool.wait_ge(s_var, n + 1)
                pool.tensor_tensor(rstd[:, NT * b:NT * b + NT], veps[:, NT * b:NT * b + NT], neghalf[:],
                                   ALU.pow).then_inc(s_rstd, 1)

            link(pool.memset(neghalf[:], -0.5))
            pool.memset(V2s[:], 0.0).then_inc(s_vpad, 1)
            pool.memset(Vs[0][:], 0.0).then_inc(s_vpad, 1)
            rstd_of(0, 0)
            link(pool.memset(maskb[:], 0.0))
            pool.affine_select(out=maskb[:], in_=maskb[:], compare_op=ALU.is_ge, fill=-1e30, base=0,
                               pattern=[[-1, P]], channel_multiplier=1).then_inc(s_const, 1)
            pool.wait_ge(s_vpad, 2)
            pool.memset(V2s[:, :, :, HD:HD + 1], 1.0).then_inc(s_vpad, 1)
            pool.memset(Vs[0][:, :, :, HD:HD + 1], 1.0).then_inc(s_vpad, 1)
            rstd_of(1, 1)
            pool.memset(Vs[1][:], 0.0).then_inc(s_vpad, 1)
            pool.wait_ge(s_vpad, 5)
            pool.memset(Vs[1][:, :, :, HD:HD + 1], 1.0).then_inc(s_vpad, 1)
            for i, width in ((1, S), (2, B * MP)):
                pool.wait_ge(s_kfull, i + 1)
                if i == 2:
                    pool.wait_ge(s_kscr, 16)
                split(pool, link, kparts[i % 2][:, :, 0:width], full[2][:, 0:width], rest[2][:, 0:width])\
                    .then_inc(s_kparts[i], 1)
                pool.wait_ge(s_kparts[i], 1)
            link(pool.memset(ones[:], 1.0))

            def scores(n, i):
                if KIND(n) == "cross":
                    return
                at, width, blocks = exp_units("self")[i]
                pool.wait_ge(s_exp, ST_FIRST[n] + i + 1)
                nb = len(blocks)
                if nb == 1:
                    v = prob[n % 2][:, at:at + P].unsqueeze(1)
                else:
                    step = blocks[1][2]
                    v = prob[n % 2][:, at:at + S].rearrange("p (n s) -> p n s", s=P)[:, 0:step // P + 1:step // P, :]
                pool.affine_select(out=v, in_=v, compare_op=ALU.is_ge, fill=0.0, base=0,
                                   pattern=[[0, nb], [1, P]], channel_multiplier=-1).then_inc(s_causal, 1)

            def split_tokens(ln, b):
                if ln == 2:
                    pool.wait_ge(s_xn, 2 * B + b + 1)
                    split(pool, link, xns[b], xn[:, b], rest[2][:].rearrange("p (t c) -> p t c", t=NT))\
                        .then_inc(s_xns, 1)

            def split_probs(b):
                pool.wait_ge(s_pr, b + 1)
                split(pool, link, prs[b], pr[b][:], pr_rest[:]).then_inc(s_prs, 1)

            play({"scores": scores, "xnT": split_tokens, "choice": split_probs,
                  "norm": lambda i: rstd_of(B + i, i % B)})

        @block.scalar
        def _(act):
            def copy_xnT(i, b, bank):
                act.wait_ge(s_xnTp, i + 1)
                act.copy(xnT[:, b], bank[:]).then_inc(s_xnT, 1)

            def copy_values(b):
                act.wait_ge(s_vp, b + 1)
                act.wait_ge(s_vpad, 4 + 2 * b)
                act.copy(Vs[b][:, :, :, 0:HD], v_banks[b][:].rearrange("p (t h d) -> p t h d", t=NT, d=HD))\
                    .then_inc(s_v, 1)

            def copy_keys(i, width):
                act.wait_ge(s_kp, i + 1)
                if i == 2:
                    act.wait_ge(s_kparts[1], 1)
                if i < B:
                    act.copy(full[1 + i][:, 0:width], k_banks[i][:, 0:width]).then_inc(s_kfull, 1)
                else:
                    act.activation(full[2][:, 0:width], k_banks[i][:, 0:width], ACT.Identity, bias=bk_sb[:, 0:1])\
                        .then_inc(s_kfull, 1)

            for b in range(B):
                copy_xnT(b, b, ps[2 + b])
                copy_keys(b, S)
                copy_values(b)
            act.wait_ge(s_vp, 3)
            for b in range(B):
                act.copy(V2s[:, b, :, 0:HD], v_banks[2][0:M, b * C:(b + 1) * C].rearrange("p (h d) -> p h d", d=HD))\
                    .then_inc(s_v, 1)
            act.wait_ge(s_late, 32)
            copy_keys(2, B * MP)

            def negmax_out(n):
                act.wait_ge(s_nmTp, n + 1)
                if n >= 2:
                    act.wait_ge(s_nmrow[n % 2], 16 * (n // 2))
                act.copy(nmT[n % 2][:], tp_bank[:].bitcast(BF16)[0:2 * G, 0:S]).then_inc(s_nmT, 1)

            def scores(n, i):
                rows = P if KIND(n) == "self" else M
                at, width, blocks = exp_units(KIND(n))[i]
                seq = ST_FIRST[n] + i
                act.wait_ge(s_st, seq + 1)
                if n >= 2:
                    act.wait_ge(s_pv, n - 1)
                act.activation(prob[n % 2][0:rows, at:at + width], st_banks[seq % STB][0:rows, 0:width],
                               ACT.Exp).then_inc(s_exp, 1)

            def values_out(n):
                act.wait_ge(s_pv, n + 1)
                if n >= 2:
                    act.wait_ge(s_oTp, n - 1)
                act.copy(oT[n % 2][:], pv_bank[:]).then_inc(s_oT, 1)

            def hidden_mlp(b, j):
                act.wait_ge(s_h1p, 2 * b + j + 1)
                act.activation(h1[b][:, j], tp_bank[:], ACT.Relu, bias=b1_sb[:, j:j + 1]).then_inc(s_h1, 1)

            def gate(b):
                act.wait_ge(s_gz, b + 1)
                act.activation(pr[b][:], pr[b][:], ACT.Exp).then_inc(s_gexp, 1)

            def turn(k):
                act.wait_ge(s_turn, k + 1)
                if k >= 2:
                    act.wait_ge(s_comb, k - 1)
                act.copy(scatter[k % 2][:], turn_bank[:].bitcast(BF16)[:, 0:S]).then_inc(s_scatter, 1)

            def experts_hidden(k):
                act.wait_ge(s_hid, k + 1)
                if k >= 2:
                    act.wait_ge(s_yp, k - 1)
                act.activation(hidden[k % 2], hid_banks[k % 2][:], ACT.Gelu).then_inc(s_gelu, 1)

            def experts_out(k):
                act.wait_ge(s_yp, k + 1)
                act.wait_ge(s_pslot, k + 1)
                if k >= 2:
                    act.wait_ge(s_comb, k - 1)
                act.activation(ys[k % 2][:, 0], y_bank[:, 0:C], ACT.Copy, scale=pslot[k % 2][:, 0:1])\
                    .then_inc(s_yhi, 1)

            def gathered(b):
                act.wait_ge(s_comb, E * (b + 1))
                act.copy(combT[b][:], comb_bank[:]).then_inc(s_combT, 1)

            play({"negrow": negmax_out, "combined": gathered, "scores": scores, "values_out": values_out,
                  "xnT": lambda ln, b: copy_xnT(B * ln + b, b, tp_bank), "hidden": hidden_mlp, "gate": gate,
                  "turn": turn, "experts_hidden": experts_hidden, "experts_out": experts_out})

        @block.vector
        def _(dve):
            links = 0

            def link(ins):
                nonlocal links
                links += 1
                ins.then_inc(s_dve, 1)
                dve.wait_ge(s_dve, links)

            def statistics(b):
                for t in range(NT):
                    ins = dve.bn_stats(stats[:, t], x_sb[:, b, t])
                link(ins)
                for t in range(NT):
                    ins = dve.bn_aggr(mv[:, NT * b + t], stats[:, t])
                link(ins)
                dve.tensor_scalar(veps[:, NT * b:NT * b + NT], mv[:, NT * b:NT * b + NT, 1], EPS, None, ALU.add)\
                    .then_inc(s_var, 1)

            def normalise_tokens(n, b):
                dve.wait_ge(s_rstd, n + 1)
                for t in range(NT):
                    i = NT * b + t
                    ins = dve.tensor_scalar(xn[:, b, t], x_sb[:, b, t], mv[:, i, 0:1], rstd[:, i:i + 1],
                                            ALU.subtract, ALU.mult)
                ins.then_inc(s_xn, 1)
                dve.wait_ge(s_xn, n + 1)

            def split_queries(i, bank, bias):
                dve.wait_ge(s_qp, i + 1)
                f = full[0][:]
                if i >= 2:
                    dve.wait_ge(s_qscr, 16 * (i - 1))
                dve.tensor_scalar(f, bank[:], bias, SCALE, ALU.add, ALU.mult).then_inc(s_qfull, 1)
                dve.wait_ge(s_qfull, i + 1)
                split(dve, link, qparts[i % 2], f, rest[0][:]).then_inc(s_qparts, 1)

            dve.wait_ge(s_x[0], 16)
            statistics(0)
            normalise_tokens(0, 0)
            dve.wait_ge(s_first, 16)
            dve.tensor_copy(identb[:], ident_sb).then_inc(s_identb, 1)
            dve.wait_ge(s_x[1], 16)
            statistics(1)
            normalise_tokens(1, 1)
            dve.wait_ge(s_kfull, 1)
            split(dve, link, kparts[0], full[1][:], rest[1][:]).then_inc(s_kparts[0], 1)
            for b in range(B):
                split_queries(b, q_banks[b], 0.0)
            dve.wait_ge(s_v, 2 * B)
            dve.wait_ge(s_late, 32)
            for b in range(B):
                v = V2s[:, b, :, 0:HD]
                dve.tensor_tensor(v, v, bv_sb.rearrange("p (h d) -> p h d", d=HD), ALU.add).then_inc(s_v2, 1)

            def maxima(n, i):
                t, heads, keys = max_units(KIND(n))[i]
                seq = MX_FIRST[n] + i
                dve.wait_ge(s_mx, seq + 1)
                bank = mx_banks[seq % MXB][:, 0:len(heads) * keys].rearrange("p (h k) -> p h k", k=keys)
                dve.tensor_reduce(nmax[n % 2][:, t, heads[0]:heads[0] + len(heads)], bank, AX.X, ALU.max,
                                  negate=True).then_inc(s_mxfree, 1)

            def negmax(n):
                dve.wait_ge(s_mxfree, MX_FIRST[n + 1])
                if n >= 2:
                    dve.wait_ge(s_nmTp, n - 1)
                link(dve.tensor_copy(nmp[n % 2][:, :, 0, :], nmax[n % 2][:]))
                dve.tensor_tensor(nmp[n % 2][:, :, 1, :], nmax[n % 2][:], nmp[n % 2][:, :, 0, :], ALU.subtract)\
                    .then_inc(s_nmp, 1)

            def output(n):
                kind, b, g = GROUPS[n]
                dve.wait_ge(s_oTp, n + 1)
                tp = tp_bank[:].rearrange("p (t h w) -> p t h w", t=NT, w=VW)
                link(dve.reciprocal(rden[:], tp[:, :, :, HD]))
                w = G * HD
                o = on[b][:, :, w * g:w * g + w].rearrange("p t (h d) -> p t h d", d=HD)
                dve.tensor_tensor(o, tp[:, :, :, 0:HD], rden[:].unsqueeze(3).to_broadcast([P, NT, G, HD]),
                                  ALU.mult).then_inc(s_on, 1)
                dve.wait_ge(s_on, n + 1)

            def copy_onT(i):
                dve.wait_ge(s_onTp, i + 1)
                dve.tensor_copy(onT[:], tp_bank[:]).then_inc(s_onT, 1)

            def add_residual(i, b):
                dve.wait_ge(s_resp, i + 1)
                xb = x_sb[:, b].rearrange("p t c -> p (t c)")
                dve.tensor_tensor(xb, tp_bank[:], xb, ALU.add).then_inc(s_res, 1)
                dve.wait_ge(s_res, i + 1)
                if i >= B:
                    link(dve.tensor_tensor(x_sb[:, b], x_sb[:, b], b2_sb.unsqueeze(1).to_broadcast([P, NT, C]),
                                           ALU.add))
                statistics(b)

            def gate(b):
                dve.wait_ge(s_gate, b + 1)
                z = tp_bank[:, 0:NT * E].rearrange("p (n e) -> p n e", e=E)
                link(dve.tensor_reduce(gmax[:], z, AX.X, ALU.max))
                dve.tensor_tensor(pr[b][:], z, gmax[:].unsqueeze(2).to_broadcast([P, NT, E]), ALU.subtract)\
                    .then_inc(s_gz, 1)

            def probs(b):
                dve.wait_ge(s_gexp, b + 1)
                link(dve.tensor_reduce(gsum[:], pr[b][:], AX.X, ALU.add))
                link(dve.reciprocal(gsum[:], gsum[:]))
                dve.tensor_tensor(pr[b][:], pr[b][:], gsum[:].unsqueeze(2).to_broadcast([P, NT, E]), ALU.mult)\
                    .then_inc(s_pr, 1)
                dve.wait_ge(s_pr, b + 1)

            def choice(b):
                dve.wait_ge(s_prT, b + 1)
                dve.tensor_copy(work[b], tp_bank[0:E, :]).then_inc(s_work, 1)
                dve.wait_ge(s_work, b + 1)

            def top(b, r):
                link(dve.max(top8[:], work[b]))
                link(dve.match_replace(work[b], top8[:], work[b], -1.0))

            def slots(b):
                link(dve.tensor_scalar(sel[b], work[b], 0.0, None, ALU.is_lt))
                link(dve.tensor_tensor_scan(slot[b], sel[b], ones[:], 0.0, ALU.add, ALU.mult))
                dve.tensor_tensor(slot[b], slot[b], sel[b], ALU.mult).then_inc(s_slot, 1)

            def slotsT(b):
                dve.wait_ge(s_slotT, b + 1)
                dve.tensor_copy(slT[b][:], tp_bank[:, 0:NT * E].rearrange("p (t n) -> p t n", t=NT)).then_inc(s_slT, 1)
                dve.wait_ge(s_slT, b + 1)

            def choose(k):
                b, e = divmod(k, E)
                if k >= 2:
                    dve.wait_ge(s_turn, k - 1)
                dve.tensor_tensor(onehot[k % 2][:], iota_sb.unsqueeze(1).to_broadcast([P, NT, CAP]),
                                  slT[b][:, :, e:e + 1].to_broadcast([P, NT, CAP]), ALU.is_equal)\
                    .then_inc(s_onehot, 1)

            def gather(k):
                dve.wait_ge(s_gather, k + 1)
                if k >= 2:
                    dve.wait_ge(s_hid, k - 1)
                bank = gather_banks[k % 2]
                dve.tensor_copy(xin[k % 2], bank[:, 0:CAP]).then_inc(s_xin, 1)
                if k >= 2:
                    dve.wait_ge(s_y, k - 1)
                dve.tensor_reduce(pslot[k % 2][:], bank[:, CAP:CAP + PARTS], AX.X, ALU.add).then_inc(s_pslot, 1)

            def experts_out(k):
                dve.wait_ge(s_yhi, k + 1)
                dve.wait_ge(s_pslot, k + 1)
                dve.scalar_tensor_tensor(ys[k % 2][:, 1], y_bank[:, 0:C], pslot[k % 2][:, 0:1], ys[k % 2][:, 0],
                                         ALU.mult, ALU.subtract).then_inc(s_y, 1)

            def finish(b):
                dve.wait_ge(s_combTp, b + 1)
                xb = x_sb[:, b].rearrange("p t c -> p (t c)")
                dve.tensor_tensor(xb, tp_bank[:], xb, ALU.add).then_inc(s_fin, 1)

            play({"max": maxima, "negmax": negmax, "output": output, "onT": copy_onT,
                  "residual": lambda b: add_residual(b, b), "mlp": lambda b: add_residual(B + b, b),
                  "q2": lambda b: split_queries(B + b, tp_bank, bq_sb[:, 0:1]),
                  "norm": lambda i: normalise_tokens(B + i, i % B), "gate": gate, "probs": probs,
                  "choice": choice, "top": top, "slots": slots, "slotsT": slotsT, "choose": choose,
                  "gather": gather, "experts_out": experts_out, "finish": finish})

        @block.tensor
        def _(pe):
            def transposed(bank, tiles):
                for t in range(NT):
                    src = tiles(t)
                    ins = pe.transpose(bank[0:src.shape[1], t * P:t * P + P], src, ident_sb)
                return ins

            pe.wait_ge(s_first, 16)
            for b in range(B):
                pe.wait_ge(s_xn, b + 1)
                transposed(ps[2 + b], lambda t: xn[:, b, t]).then_inc(s_xnTp, 1)
                pe.wait_ge(s_xnT, b + 1)
                pe.matmul(k_banks[b][:], wqkvT_sb[:, C:2 * C], xnT[:, b], start=True, stop=True).then_inc(s_kp, 1)
                pe.matmul(q_banks[b][:], wqkvT_sb[:, 0:C], xnT[:, b], start=True, stop=True).then_inc(s_qp, 1)
                for t in range(NT):
                    ins = pe.matmul(v_banks[b][:, t * C:(t + 1) * C], xnT[:, b, t * P:(t + 1) * P],
                                    wqkvT_sb[:, 2 * C:3 * C], start=True, stop=True)
                ins.then_inc(s_vp, 1)
            pe.wait_ge(s_ctxw, 16)
            pe.wait_ge(s_v, 1)
            for b in range(B):
                ins = pe.matmul(v_banks[2][0:M, b * C:(b + 1) * C], ctxT_sb[:, MP * b:MP * b + M], wv_sb, start=True,
                                stop=True)
            ins.then_inc(s_vp, 1)
            pe.wait_ge(s_kfull, 1)
            pe.matmul(k_banks[2][:, 0:B * MP], wk_sb, ctxT_sb, start=True, stop=True).then_inc(s_kp, 1)
            pe.wait_ge(s_const, 1)
            pe.wait_ge(s_identb, 1)
            pe.wait_ge(s_xnT, B)
            pe.wait_ge(s_v, 2 * B)
            pe.wait_ge(s_kfull, 3)
            pe.wait_ge(s_qfull, B)

            def operands(n):
                kind, b, g = GROUPS[n]
                if kind == "self":
                    return Qs[b][0:ROWS, G * g:G * g + G], Ks[b][0:ROWS, G * g:G * g + G]
                return Qs[b][0:ROWS, G * g:G * g + G], K2s[0:ROWS, G * g:G * g + G, MP * b:MP * b + M]

            def max_scores(n, i):
                kind, b, g = GROUPS[n]
                q, k = operands(n)
                t, heads, keys = max_units(kind)[i]
                seq = MX_FIRST[n] + i
                if i == 0:
                    if kind == "self":
                        pe.wait_ge(s_qstack[b], 16 * PARTS)
                        pe.wait_ge(s_kstack[b], 16 * PARTS)
                        pe.wait_ge(s_fixed[b], 32)
                    else:
                        pe.wait_ge(s_qstack[B + b], 16 * PARTS)
                        pe.wait_ge(s_kstack[B], 16 * PARTS)
                        pe.wait_ge(s_fixed2, 16)
                if seq >= MXB:
                    pe.wait_ge(s_mxfree, seq - MXB + 1)
                bank = mx_banks[seq % MXB]
                for j, h in enumerate(heads):
                    ins = pe.matmul(bank[:, j * keys:(j + 1) * keys], q[0:MAXROW, h, t * P:(t + 1) * P],
                                    k[0:MAXROW, h, 0:keys], start=(j == 0), stop=(kind == "cross"),
                                    skip_group_check=True)
                    if kind == "self":
                        ins = pe.matmul(bank[:, (j + 1) * keys - P:(j + 1) * keys], identb[:], maskb[:],
                                        start=False, stop=True, skip_group_check=True)
                ins.then_inc(s_mx, 1)

            def negmax(n):
                pe.wait_ge(s_nmp, n + 1)
                take_tp((s_nmT, n + 1))
                for t in range(NT):
                    ins = pe.transpose(tp_bank[:].bitcast(BF16)[0:2 * G, t * P:(t + 1) * P],
                                       nmp[n % 2][:, t].rearrange("p i h -> p (i h)"), identb[:])
                ins.then_inc(s_nmTp, 1)

            def scores(n, i):
                kind, b, g = GROUPS[n]
                q, k = operands(n)
                at, width, blocks = exp_units(kind)[i]
                seq = ST_FIRST[n] + i
                if i == 0:
                    pe.wait_ge(s_nmrow[n % 2], 16 * (n // 2 + 1))
                if seq >= STB:
                    pe.wait_ge(s_exp, seq - STB + 1)
                for m, (h, j, col, qt) in enumerate(blocks):
                    rows, keys = (P, k[:, h, j * P:(j + 1) * P]) if kind == "self" else (M, k[:, h, :])
                    ins = pe.matmul(st_banks[seq % STB][0:rows, col:col + S - qt * P], keys, q[:, h, qt * P:S],
                                    start=(m == 0), stop=True, skip_group_check=True)
                ins.then_inc(s_st, 1)

            def values(n, j):
                kind, b, g = GROUPS[n]
                if j == 0:
                    if kind == "self":
                        pe.wait_ge(s_causal, ST_FIRST[n + 1])
                    else:
                        pe.wait_ge(s_exp, ST_FIRST[n + 1])
                        pe.wait_ge(s_v2, B)
                    if n > 0:
                        pe.wait_ge(s_oT, n)
                last = NT - 1 if kind == "self" else 0
                for h, at, qt in sorted((h, at + col, qt) for at, _, bl in exp_units(kind) for h, jj, col, qt in bl
                                        if jj == j):
                    v, rows = (Vs[b][:, j, G * g + h, :], P) if kind == "self" else (V2s[:, b, G * g + h, :], M)
                    ins = pe.matmul(pv_bank[VW * h:VW * h + VW, qt * P:S], v,
                                    prob[n % 2][0:rows, at:at + S - qt * P], start=(j == 0), stop=(j == last),
                                    tile_position=(0, VW * h), skip_group_check=True)
                if j == last:
                    ins.then_inc(s_pv, 1)

            tp_user = None

            def take_tp(user):
                nonlocal tp_user
                if tp_user:
                    pe.wait_ge(*tp_user)
                tp_user = user

            def output(n):
                pe.wait_ge(s_oT, n + 1)
                take_tp((s_on, n + 1))
                transposed(tp_bank, lambda t: oT[n % 2][:, t * P:(t + 1) * P]).then_inc(s_oTp, 1)

            def turn_on(i):
                pe.wait_ge(s_on, NG * (i + 1))
                take_tp((s_onT, i + 1))
                transposed(tp_bank, lambda t: on[i % B][:, t]).then_inc(s_onTp, 1)

            def residual(b):
                pe.wait_ge(s_late, 32)
                pe.wait_ge(s_onT, b + 1)
                take_tp((s_res, b + 1))
                for t in range(NT):
                    ins = pe.matmul(tp_bank[:, t * C:(t + 1) * C], onT[:, t * P:(t + 1) * P], woT_sb, start=True,
                                    stop=True)
                ins.then_inc(s_resp, 1)

            def turn_xn(ln, b):
                i = B * ln + b
                pe.wait_ge(s_xn, i + 1)
                take_tp((s_xnT, i + 1))
                transposed(tp_bank, lambda t: xn[:, b, t]).then_inc(s_xnTp, 1)

            def q2(b):
                pe.wait_ge(s_xnT, B + b + 1)
                take_tp((s_qfull, B + b + 1))
                pe.matmul(tp_bank[:], wq_sb, xnT[:, b], start=True, stop=True).then_inc(s_qp, 1)

            def hidden_mlp(b, j):
                pe.wait_ge(s_onT, B + b + 1)
                take_tp((s_h1, 2 * b + j + 1))
                pe.matmul(tp_bank[:], w1_sb[:, j * C:(j + 1) * C], onT[:], start=True, stop=True).then_inc(s_h1p, 1)

            def mlp(b):
                pe.wait_ge(s_h1, 2 * b + 2)
                take_tp((s_res, B + b + 1))
                for t in range(NT):
                    for j in range(2):
                        ins = pe.matmul(tp_bank[:, t * C:(t + 1) * C], h1[b][:, j, t * P:(t + 1) * P],
                                        w2_sb[:, j * C:(j + 1) * C], start=(j == 0), stop=(j == 1),
                                        skip_group_check=True)
                ins.then_inc(s_resp, 1)

            def gate(b):
                pe.wait_ge(s_xnT, 2 * B + b + 1)
                take_tp((s_gz, b + 1))
                for t in range(NT):
                    ins = pe.matmul(tp_bank[:, t * E:(t + 1) * E], xnT[:, b, t * P:(t + 1) * P], gw_sb, start=True,
                                    stop=True)
                ins.then_inc(s_gate, 1)

            def choice(b):
                pe.wait_ge(s_pr, b + 1)
                take_tp((s_work, b + 1))
                transposed(tp_bank, lambda t: pr[b][:, t]).then_inc(s_prT, 1)

            def slots(b):
                pe.wait_ge(s_slot, b + 1)
                take_tp((s_slT, b + 1))
                for t in range(NT):
                    ins = pe.transpose(tp_bank[:, t * E:(t + 1) * E], slot[b][:, t * P:(t + 1) * P],
                                       ident_sb[0:E, 0:E])
                ins.then_inc(s_slotT, 1)

            def gather(k):
                b, e = divmod(k, E)
                pe.wait_ge(s_onehot, k + 1)
                pe.wait_ge(s_xns, b + 1)
                pe.wait_ge(s_prs, b + 1)
                if k >= 2:
                    pe.wait_ge(s_pslot, k - 1)
                bank = gather_banks[k % 2]
                for t in range(NT):
                    for i in range(PARTS):
                        pe.matmul(bank[:, 0:CAP], xns[b][:, i, t], onehot[k % 2][:, t], start=(t == 0 and i == 0),
                                  stop=(t == NT - 1 and i == PARTS - 1), skip_group_check=True)
                for t in range(NT):
                    ins = pe.matmul(bank[:, CAP:CAP + PARTS], onehot[k % 2][:, t], prs[b][:, :, t, e],
                                    start=(t == 0), stop=(t == NT - 1), skip_group_check=True)
                ins.then_inc(s_gather, 1)

            def turn(k):
                if k >= 1:
                    pe.wait_ge(s_scatter, k)
                for t in range(NT):
                    ins = pe.transpose(turn_bank[:].bitcast(BF16)[:, t * P:(t + 1) * P], onehot[k % 2][:, t],
                                       identb[:])
                ins.then_inc(s_turn, 1)

            def experts_hidden(k):
                b, e = divmod(k, E)
                if k == 0:
                    pe.wait_ge(s_moew, 64)
                pe.wait_ge(s_xin, k + 1)
                if k >= 2:
                    pe.wait_ge(s_gelu, k - 1)
                for c in range(NC):
                    ins = pe.matmul(hid_banks[k % 2][:, c * CAP:(c + 1) * CAP], mw1_sb[:, e, c * P:(c + 1) * P],
                                    xin[k % 2], start=(c == 0), stop=True, skip_group_check=True)
                ins.then_inc(s_hid, 1)

            def experts_out(k):
                b, e = divmod(k, E)
                pe.wait_ge(s_gelu, k + 1)
                if k >= 1:
                    pe.wait_ge(s_y, k)
                for c in range(NC):
                    ins = pe.matmul(y_bank[:, 0:C], hidden[k % 2][:, c * CAP:(c + 1) * CAP], mw2_sb[:, e, c],
                                    start=(c == 0), stop=(c == NC - 1))
                ins.then_inc(s_yp, 1)

            def combine(k):
                b, e = divmod(k, E)
                pe.wait_ge(s_y, k + 1)
                pe.wait_ge(s_scatter, k + 1)
                if e == 0 and b:
                    pe.wait_ge(s_combT, b)
                for i in range(2):
                    ins = pe.matmul(comb_bank[:], ys[k % 2][:, i], scatter[k % 2][:], start=(e == 0 and i == 0),
                                    stop=(e == E - 1 and i == 1))
                ins.then_inc(s_comb, 1)

            def finish(b):
                pe.wait_ge(s_combT, b + 1)
                take_tp((s_fin, b + 1))
                transposed(tp_bank, lambda t: combT[b][:, t * P:(t + 1) * P]).then_inc(s_combTp, 1)

            play({"finish": finish, "max": max_scores, "negrow": negmax, "scores": scores, "values": values, "output": output,
                  "onT": turn_on, "residual": residual, "xnT": turn_xn, "q2": q2, "hidden": hidden_mlp, "mlp": mlp,
                  "gate": gate, "choice": choice, "slotsT": slots, "gather": gather, "turn": turn, "experts_hidden": experts_hidden,
                  "experts_out": experts_out, "combine": combine})



def bf16_parts(v):
    out = []
    for _ in range(PARTS):
        hi = (v.view(np.uint32) & np.uint32(0xFFFF0000)).view(np.float32)
        out.append((hi.view(np.uint32) >> 16).astype(np.uint16))
        v = (v - hi).astype(np.float32)
    return np.stack(out)


def fixed_rows(rows, width):
    out = np.zeros((ROWS - SLOT_ROWS, H, width), np.uint16)
    for row, bits in rows:
        out[row - SLOT_ROWS] = bits
    return out


def shape_constants():
    slopes = np.float32([(2.0 ** -0.5) ** (i + 1) for i in range(H)])
    alibi = bf16_parts(np.ascontiguousarray(-(slopes[:, None] * np.arange(S, dtype=np.float32)[None, :])))
    one = np.uint16(0x3F80)
    return {
        "k_fixed": fixed_rows([(ALIBI + i, alibi[i]) for i in range(PARTS)] + [(MAXROW, one), (MAXROW + 1, one)], S),
        "q_fixed": fixed_rows([(ALIBI + i, one) for i in range(PARTS)], S),
        "k2_fixed": fixed_rows([(MAXROW, one), (MAXROW + 1, one)], B * MP),
    }


def kernel(x, ctx_768, L0_attn_W_qkv, L0_attn_W_o, L0_xattn_Wq, L0_xattn_bq, L0_xattn_Wk, L0_xattn_bk,
           L0_xattn_Wv, L0_xattn_bv, L0_xattn_W1, L0_xattn_b1, L0_xattn_W2, L0_xattn_b2, L0_ffn_gate_w,
           L0_ffn_w1, L0_ffn_w2):
    import concourse.bacc as bacc
    from concourse.bass_utils import run_bass_kernel_spmd

    a = np.asarray

    def channel_first(w):
        return w.reshape(w.shape[0], H, HD).transpose(0, 2, 1).reshape(w.shape[0], C)

    wqkvT = a(L0_attn_W_qkv).T
    padded = np.zeros((CT, B, MP), np.float32)
    padded[:, :, 0:M] = a(ctx_768).transpose(2, 0, 1)
    iota = np.broadcast_to(np.arange(1, P + 1, dtype=np.float32), (P, P))
    data = {
        "x": a(x),
        "first": np.concatenate([channel_first(wqkvT[:, 0:C]), channel_first(wqkvT[:, C:2 * C]),
                                 wqkvT[:, 2 * C:], np.eye(P, dtype=np.float32)], axis=1),
        "ctxw": np.concatenate([channel_first(a(L0_xattn_Wk)), a(L0_xattn_Wv), padded.reshape(CT, B * MP)], axis=1),
        "late": np.concatenate([
            a(L0_attn_W_o).T, channel_first(a(L0_xattn_Wq)), a(L0_xattn_W1),
            a(L0_xattn_W2).reshape(2, C, C).transpose(1, 0, 2).reshape(C, 2 * C), iota,
            a(L0_xattn_b1).reshape(2, C).T, channel_first(a(L0_xattn_bq)[None]).T,
            channel_first(a(L0_xattn_bk)[None]).T, a(L0_ffn_gate_w)], axis=1),
        "rows": np.concatenate([a(L0_xattn_bv), a(L0_xattn_b2)]),
        "mw1": a(L0_ffn_w1).transpose(1, 0, 2),
        "mw2": a(L0_ffn_w2).reshape(E, NC, P, C).transpose(2, 0, 1, 3),
        **shape_constants(),
    }
    nc = bacc.Bacc("TRN2", target_bir_lowering=False, num_devices=1)
    arrays, args = {}, {}
    for name, v in data.items():
        v = np.ascontiguousarray(v)
        arrays[f"in_{name}"] = v
        t = nc.dram_tensor(f"in_{name}", v.shape, mybir.dt.from_np(v.dtype), kind="ExternalInput").ap()
        args[name] = t.bitcast(BF16) if v.dtype == np.uint16 else t
    out = nc.dram_tensor("out", (B, S, C), F32, kind="ExternalOutput").ap()
    decoder_block(nc, out=out, **args)
    r = run_bass_kernel_spmd(nc, [arrays], core_ids=[0])
    return r.results[0]["out"]
```

```python
from contextlib import ExitStack

import numpy as np

import concourse.bass as bass
from concourse import mybir

F32 = mybir.dt.float32
BF16 = mybir.dt.bfloat16
F32R = mybir.dt.float32r
ALU = mybir.AluOpType
ACT = mybir.ActivationFunctionType
AX = mybir.AxisListType

P = 128
B, S, C, H = 2, 512, 128, 16
HD = C // H
NT = S // P
M, CT = 77, 96
MP = 80
E, CAP, FF = 8, 2 * S // 8, 512
NC = FF // P
G = 4
NG = H // G
SCALE = float(np.float32(HD ** -0.5))
EPS = 1e-5

PARTS = 3
SLOT_ROWS = PARTS * PARTS * HD
ALIBI = SLOT_ROWS
MAXROW = 96
ROWS = MAXROW + 2
VW = 32


def max_units(kind):
    if kind == "cross":
        return [(t, tuple(range(G)), M) for t in range(NT)]
    return ([(3, (h,), 4 * P) for h in range(G)] + [(2, (h,), 3 * P) for h in range(G)]
            + [(1, (0, 1), 2 * P), (1, (2, 3), 2 * P), (0, (0, 1, 2, 3), P)])


def exp_units(kind):
    if kind == "cross":
        return [(S * h, S, [(h, 0, 0, 0)]) for h in range(G)]
    units = []
    for a in (0, 2):
        for h in (a, a + 1):
            units.append((2 * S * h, S, [(h, 0, 0, 0)]))
            units.append((2 * S * h + S, S, [(h, 1, 0, 1), (h, 3, 3 * P, 3)]))
        units.append((2 * S * G + S * (a // 2), S, [(a, 2, 0, 2), (a + 1, 2, 2 * P, 2)]))
    return units


GROUPS = [(kind, b, g) for kind in ("self", "cross") for b in range(B) for g in range(NG)]
FIRST = (0, 8, 12)
ROUNDS = CAP // 8


def KIND(n):
    return GROUPS[n][0]


MX_FIRST, ST_FIRST = [0], [0]
for _kind, _, _ in GROUPS:
    MX_FIRST.append(MX_FIRST[-1] + len(max_units(_kind)))
    ST_FIRST.append(ST_FIRST[-1] + len(exp_units(_kind)))


WEIGHT = {"tail0": 1, "tail1": 1, "mlp0": 1, "mlp1": 1, "self_slot": 0.85, "cross_slot0": 0.85,
          "cross_slot1": 0.85, "max": 0.6, "negmax": 1, "values": 0.5, "values_out": 0.13, "pause": 0.59,
          "output": 1.01, "onT": 3.08, "residual": 1.4, "sum": 2.91, "norm": 2.53, "xnT": 2.18, "q2": 1.13,
          "q2parts": 3.11, "q2read": 5, "hidden": 1.57, "mlp": 0.97, "gate": 2.6, "probs": 1.77,
          "choice": 2.47, "top0": 1.47, "top1": 1.47, "slots": 2.1, "slotsT": 0.07, "expert0": 0.58,
          "expert1": 1.47, "weights": 7.78, "context_keys": 0.17, "finish": 0.07}
VALUE_SLOTS = (1, 2, 3, 4, 6, 8, 9)
NEGROW_DELAY = 5
LEAD_UNITS = 6


def together(streams, requires, bank_users):
    clocks, places, order, done = [0.0] * len(streams), [0] * len(streams), [], {}
    holder = None
    while True:
        choice = None
        for i, stream in enumerate(streams):
            if places[i] == len(stream):
                continue
            entry = stream[places[i]][1]
            needs = requires.get(entry, [])
            if any(need not in done for need in needs):
                continue
            if holder and holder[0] != i and entry and entry[0] in bank_users["all"]:
                continue
            at = max([clocks[i]] + [done[need] for need in needs])
            if choice is None or at < choice[0]:
                choice = (at, i)
        if choice is None:
            break
        at, i = choice
        weight, entry = streams[i][places[i]]
        places[i] += 1
        clocks[i] = at + weight
        if entry:
            order.append(entry)
            done[entry] = clocks[i]
            if holder and holder[0] == i and entry[0] == holder[1]:
                holder = None
            if entry[0] in bank_users["held"]:
                holder = (i, bank_users["held"][entry[0]])
    assert all(p == len(stream) for p, stream in zip(places, streams))
    return order


def schedule():
    def weigh(*entries):
        return [(WEIGHT[entry[0]], entry) for entry in entries]

    def maxima(n):
        return weigh(*[("max", n, i) for i in range(len(max_units(KIND(n))))])

    def finish(n):
        return weigh(*[("values", n, j) for j in range(NT if KIND(n) == "self" else 1)], ("values_out", n)) \
            + [(WEIGHT["pause"], None)] + weigh(("output", n))

    def step(n, ahead=(), lead=0):
        entries = []
        add = entries.append
        slot = WEIGHT["self_slot" if KIND(n) == "self" else f"cross_slot{GROUPS[n][1]}"]
        exp = [("scores", n, i) for i in range(len(exp_units(KIND(n))))]
        mx = [("max", m, i) for m in ahead for i in range(len(max_units(KIND(m))))][lead:]
        n_slots = max(len(exp), len(mx))
        chunks = [entry for _, entry in finish(n - 1)] if n not in FIRST else []
        for i in range(n_slots):
            if i < len(exp):
                add((slot, exp[i]))
            for _ in range(-(-len(mx) // (n_slots - i))):
                add((0 if i < len(exp) else slot, mx.pop(0)))
                m, last = entries[-1][1][1:]
                if last == len(max_units(KIND(m))) - 1:
                    add((0, ("negmax", m)))
                    pending.append([m, NEGROW_DELAY if KIND(n) == "self" else 1])
            if pending:
                pending[0][1] -= 1
                if pending[0][1] < 0:
                    add((0, ("negrow", pending.pop(0)[0])))
            if chunks and (i in VALUE_SLOTS if n_slots > 6 else i >= 1):
                add((0, chunks.pop(0)))
        entries.extend((slot / 2, c) for c in chunks)
        return entries

    def tail(b):
        return weigh(("onT", b), ("residual", b), ("sum", b), ("norm", b), ("xnT", 1, b), ("q2", b), ("q2parts", b),
                     ("q2read", b))

    def mlp(b):
        return weigh(("onT", B + b), ("hidden", b, 0), ("hidden", b, 1), ("mlp", b), ("sum", B + b),
                     ("norm", B + b), ("xnT", 2, b), ("gate", b), ("probs", b), ("choice", b))

    def selection(b):
        return [(WEIGHT[f"top{b}"], ("top", b, r)) for r in range(ROUNDS)] + weigh(("slots", b), ("slotsT", b))

    def experts(b):
        first, last = b * E, (b + 1) * E
        entries = [("choose", first), ("gather", first), ("turn", first), ("choose", first + 1)]
        for k in range(first, last):
            entries.append(("experts_hidden", k))
            if k + 2 < last:
                entries.append(("choose", k + 2))
            if k + 1 < last:
                entries.append(("gather", k + 1))
            if k > first:
                entries.append(("combine", k - 1))
            if k + 1 < last:
                entries.append(("turn", k + 1))
            entries.append(("experts_out", k))
        entries += [("combine", last - 1), ("combined", b)]
        return [(WEIGHT[f"expert{b}"], entry) for entry in entries]

    def beginning(n):
        return maxima(n) + weigh(("negmax", n)) + [(0, ("negrow", n))]

    pending = []
    attention = maxima(0) + weigh(("negmax", 0)) + maxima(1)[0:LEAD_UNITS]
    attention[3 - LEAD_UNITS:3 - LEAD_UNITS] = [(0, ("negrow", 0)), (0, ("second_batch", 0))]
    attention += step(0, [1, 2], LEAD_UNITS) + [(0, ("second_batch", 1)), (0, ("context_keys",))]
    for n in range(1, 2 * NG - 2):
        attention += step(n, [n + 2])
    attention += step(6) + step(7) + finish(7)
    for n in (8, 12):
        attention += step(n, [n + 2]) + step(n + 1, [n + 3]) + step(n + 2) + step(n + 3) + finish(n + 3)
    chains = [[(weight * WEIGHT[f"tail{b}"], entry) for weight, entry in tail(b)]
              + [(weight * WEIGHT[f"mlp{b}"], entry) for weight, entry in mlp(b)]
              + selection(b) + weigh(("finish", b)) for b in range(B)]
    requires = {("onT", 0): [("output", 3)], ("onT", 1): [("output", 7)], ("max", 8, 0): [("q2read", 0), ("negmax", 7)],
                ("max", 12, 0): [("q2read", 1), ("negmax", 11)], ("onT", 2): [("output", 11), ("q2parts", 1)],
                ("onT", 3): [("output", 15), ("choice", 0)], ("weights", 0): [("output", 7)],
                ("choose", 0): [("slotsT", 0)], ("choose", E): [("slotsT", 1)],
                ("finish", 0): [("combined", 0)], ("finish", 1): [("combined", 1)],
                ("experts_hidden", 0): [("weights", 3)]}
    for n in (8, 12):
        requires[("scores", n, 0)] = [("negrow", n), ("negmax", n + 1)]
        requires[("scores", n + 1, 0)] = [("negrow", n + 1)]
    bank_users = {"held": {"residual": "sum", "mlp": "sum", "q2": "q2parts"},
                  "all": ("onT", "residual", "xnT", "q2", "hidden", "mlp", "gate", "choice", "slotsT", "finish")}
    return together([attention + experts(0) + experts(1)] + chains + [weigh(*[("weights", i) for i in range(4)])]
                    + [beginning(n) + beginning(n + 1) for n in (8, 12)],
                    requires, bank_users)


ORDER = schedule()


def play(handlers):
    for what, *args in ORDER:
        if what in handlers:
            handlers[what](*args)


def split(engine, link, parts, value, rest):
    link(engine.tensor_copy(parts[:, 0], value))
    link(engine.tensor_tensor(rest, value, parts[:, 0], ALU.subtract))
    link(engine.tensor_copy(parts[:, 1], rest))
    return engine.tensor_tensor(parts[:, 2], rest, parts[:, 1], ALU.subtract)


def decoder_block(nc, x, first, ctxw, late, rows, k_fixed, q_fixed, k2_fixed, mw1, mw2, out):
    MXB, STB = 3, 2
    ctx = ExitStack()
    with ctx:
        def sb(name, shape, dt=F32):
            return ctx.enter_context(nc.sbuf_tensor(name, shape, dt))

        def sem(name):
            return ctx.enter_context(nc.semaphore(name))

        def cut(tile, *widths):
            at, res = 0, []
            for w in widths:
                res.append(tile[:, at:at + w])
                at += w
            return res

        ps = [ctx.enter_context(nc.psum_tensor(f"bank{i}", [P, 512], F32)) for i in range(8)]
        mx_banks = [ps[2], ps[3], ps[7]]
        st_banks = [ps[4], ps[5]]
        pv_bank, tp_bank, tail_bank = ps[0], ps[1], ps[6]
        gather_banks, hid_banks, turn_bank, y_bank, comb_bank = [ps[2], ps[3]], [ps[5], ps[1]], ps[4], ps[7], ps[0]

        x_sb = sb("x_sb", [P, B, NT, C])
        xn = sb("xn", [P, B, NT, C])
        xnT = sb("xnT", [P, B, S])
        stats = sb("stats", [P, NT, 6])
        mv = sb("mv", [P, B * NT, 2])
        veps = sb("veps", [P, B * NT])
        rstd = sb("rstd", [P, B * NT])
        neghalf = sb("neghalf", [P, NT])
        first_sb = sb("first_sb", [P, 4 * C])
        wqkvT_sb, ident_sb = cut(first_sb, 3 * C, C)
        ctxw_sb = sb("ctxw_sb", [CT, 2 * C + B * MP])
        wk_sb, wv_sb, ctxT_sb = cut(ctxw_sb, C, C, B * MP)
        late_sb = sb("late_sb", [P, 7 * C + 4 + E])
        woT_sb, wq_sb, w1_sb, w2_sb, iota_sb, b1_sb, bq_sb, bk_sb, gw_sb = cut(
            late_sb, C, C, 2 * C, 2 * C, C, 2, 1, 1, E)
        rows_sb = sb("rows_sb", [P, 2 * C])
        bv_sb, b2_sb = rows_sb[0:M, 0:C], rows_sb[:, C:2 * C]
        identb = sb("identb", [P, P], BF16)
        maskb = sb("maskb", [P, P], BF16)
        full = [sb(f"full{i}", [P, S]) for i in range(4)]
        rest = [sb(f"rest{i}", [P, S]) for i in range(3)]
        qparts = [sb(f"qparts{i}", [P, PARTS, S], BF16) for i in range(2)]
        kparts = [sb(f"kparts{i}", [P, PARTS, S], BF16) for i in range(2)]
        Qs = [sb(f"Qs{b}", [P, H, S], BF16) for b in range(B)]
        Ks = [sb(f"Ks{b}", [P, H, S], BF16) for b in range(B)]
        K2s = sb("K2s", [P, H, B * MP], BF16)
        Vs = [sb(f"Vs{b}", [P, NT, H, VW]) for b in range(B)]
        V2s = sb("V2s", [M, B, H, VW])
        prob = [sb(f"prob{i}", [P, 5 * 2 * S]) for i in range(2)]
        nmax = [sb(f"nmax{i}", [P, NT, G]) for i in range(2)]
        nmp = [sb(f"nmp{i}", [P, NT, 2, G], BF16) for i in range(2)]
        nmT = [sb(f"nmT{i}", [2 * G, S], BF16) for i in range(2)]
        oT = [sb(f"oT{i}", [P, S]) for i in range(2)]
        rden = sb("rden", [P, NT, G])
        on = [sb(f"on{b}", [P, NT, C]) for b in range(B)]
        onT = [sb(f"onT{b}", [P, S]) for b in range(B)]
        full_k2 = onT[0][:, 0:B * MP]
        mw1_sb = Ks[0][:].rearrange("p h s -> p (h s)").bitcast(F32).rearrange("p (e f) -> p e f", e=E)
        mw2_sb = Ks[1][:].rearrange("p h s -> p (h s)").bitcast(F32).rearrange("p (e c n) -> p e c n", e=E, c=NC)
        q32 = [Qs[b][:].rearrange("p h s -> p (h s)").bitcast(F32) for b in range(B)]
        h1 = [q32[b][:, 0:2 * S].rearrange("p (j s) -> p j s", j=2) for b in range(B)]
        work, sel, slot = ([q32[b][0:E, i * S:(i + 1) * S] for b in range(B)] for i in (2, 3, 4))
        ones = sb("ones", [E, S])
        top8 = sb("top8", [E, 8])
        gmax = sb("gmax", [P, NT])
        gsum = sb("gsum", [P, NT])
        pr = [sb(f"pr{b}", [P, NT, E]) for b in range(B)]
        pr_rest = sb("pr_rest", [P, NT, E])
        prs = [sb(f"prs{b}", [P, PARTS, NT, E], BF16) for b in range(B)]
        xns = [sb(f"xns{b}", [P, PARTS, NT, C], BF16) for b in range(B)]
        onehot = [sb(f"onehot{i}", [P, NT, CAP], BF16) for i in range(2)]
        scatter = [sb(f"scatter{i}", [P, S], F32R) for i in range(2)]
        ys = [sb(f"ys{i}", [P, 2, C], F32R) for i in range(2)]
        slT = [sb(f"slT{b}", [P, NT, E]) for b in range(B)]
        pslot = [sb(f"pslot{i}", [P, 1]) for i in range(2)]
        combT = [oT[b] for b in range(B)]
        hidden = [prob[0][:, i * S:(i + 1) * S] for i in range(2)]
        xin = [prob[1][:, i * CAP:(i + 1) * CAP] for i in range(2)]
        yf = [prob[1][:, 2 * CAP + i * C:2 * CAP + (i + 1) * C] for i in range(2)]

        q_scr = [nc.dram_tensor(f"q_scr{i}", (PARTS, HD * H, S), BF16, kind="Internal").ap() for i in range(2 * B)]
        k_scr = [nc.dram_tensor(f"k_scr{b}", (PARTS, HD * H, S), BF16, kind="Internal").ap() for b in range(B)]
        k2_scr = nc.dram_tensor("k2_scr", (PARTS, HD * H, B * MP), BF16, kind="Internal").ap()

        s_x = [sem(f"s_x{b}") for b in range(B)]
        s_first = sem("s_first")
        s_ctxw = sem("s_ctxw")
        s_late = sem("s_late")
        s_moew = sem("s_moew")
        s_const = sem("s_const")
        s_fixed = [sem(f"s_fixed{b}") for b in range(B)]
        s_fixed2 = sem("s_fixed2")
        s_vpad = sem("s_vpad")
        s_dve = sem("s_dve")
        s_pool = sem("s_pool")
        s_identb = sem("s_identb")
        s_var = sem("s_var")
        s_rstd = sem("s_rstd")
        s_xn = sem("s_xn")
        s_centred = sem("s_centred")
        s_norm = sem("s_norm")
        s_b2 = sem("s_b2")
        s_xnTp = sem("s_xnTp")
        s_xnT = sem("s_xnT")
        s_qp = sem("s_qp")
        s_kp = sem("s_kp")
        s_vp = sem("s_vp")
        s_qfull = sem("s_qfull")
        s_q2full = sem("s_q2full")
        s_kfull = sem("s_kfull")
        s_qparts = sem("s_qparts")
        s_kparts = [sem(f"s_kparts{i}") for i in range(B + 1)]
        s_qscr = sem("s_qscr")
        s_kscr = sem("s_kscr")
        s_qstack = [[sem(f"s_qstack{i}_{half}") for half in range(2)] for i in range(2 * B)]
        s_kstack = [[sem(f"s_kstack{i}_{half}") for half in range(2)] for i in range(B + 1)]
        s_v = sem("s_v")
        s_v2 = sem("s_v2")
        s_mx = sem("s_mx")
        s_mxfree = sem("s_mxfree")
        s_nmp = sem("s_nmp")
        s_nmTp = sem("s_nmTp")
        s_nmT = sem("s_nmT")
        s_nmrow = [sem(f"s_nmrow{i}") for i in range(2)]
        s_st = sem("s_st")
        s_exp = sem("s_exp")
        s_causal = sem("s_causal")
        s_pv = sem("s_pv")
        s_oT = sem("s_oT")
        s_oTp = sem("s_oTp")
        s_on = sem("s_on")
        s_onTp = sem("s_onTp")
        s_onT = sem("s_onT")
        s_resp = sem("s_resp")
        s_res = sem("s_res")
        s_h1p = sem("s_h1p")
        s_h1 = sem("s_h1")
        s_xns = sem("s_xns")
        s_gate = sem("s_gate")
        s_gz = sem("s_gz")
        s_gexp = sem("s_gexp")
        s_pr = sem("s_pr")
        s_prs = sem("s_prs")
        s_prT = sem("s_prT")
        s_work = sem("s_work")
        s_slot = sem("s_slot")
        s_slotT = sem("s_slotT")
        s_slT = sem("s_slT")
        s_onehot = sem("s_onehot")
        s_gather = sem("s_gather")
        s_xin = sem("s_xin")
        s_pslot = sem("s_pslot")
        s_turn = sem("s_turn")
        s_scatter = sem("s_scatter")
        s_hid = sem("s_hid")
        s_gelu = sem("s_gelu")
        s_yp = sem("s_yp")
        s_yhi = sem("s_yhi")
        s_y = sem("s_y")
        s_comb = sem("s_comb")
        s_combT = sem("s_combT")
        s_combTp = sem("s_combTp")
        s_fin = sem("s_fin")
        s_out = sem("s_out")

        q_banks, k_banks, v_banks = (ps[4], ps[7]), (ps[5], ps[0], ps[5]), (ps[6], ps[1], ps[6])

        block = ctx.enter_context(nc.Block())

        @block.sync
        def _(sp):
            ROWS_OF_PART = PARTS * HD
            HALF = H // 2

            def write_q(i):
                sp.wait_ge(s_qparts, i + 1)
                sp.dma_start(q_scr[i].rearrange("p c s -> c p s"), qparts[i % 2][:]).then_inc(s_qscr, 16)

            def read_q(i, b, halves=(0, 1)):
                sp.wait_ge(s_qscr, 16 * (i + 1))
                if i >= B:
                    sp.wait_ge(s_st, ST_FIRST[NG * (b + 1)])
                for half in halves:
                    for p in range(PARTS):
                        src = q_scr[i][p].rearrange("(d h) s -> d h s", d=HD)[:, HALF * half:HALF * (half + 1)]
                        src = src.rearrange("d h s -> d (h s)").unsqueeze(0).to_broadcast([PARTS, HD, HALF * S])
                        dst = Qs[b][ROWS_OF_PART * p:ROWS_OF_PART * (p + 1), HALF * half:HALF * (half + 1)]
                        sp.dma_start(dst.rearrange("p h s -> p (h s)"), src).then_inc(s_qstack[i][half], 16)

            def write_k(i, scr, width):
                sp.wait_ge(s_kparts[i], 1)
                sp.dma_start(scr.rearrange("p c s -> c p s"), kparts[i % 2][:, :, 0:width]).then_inc(s_kscr, 16)

            def read_k(i, tile, scr, halves=(0, 1)):
                sp.wait_ge(s_kscr, 16 * (i + 1))
                src = scr.rearrange("p (d h) s -> (p d) h s", d=HD)
                for half in halves:
                    heads = slice(HALF * half, HALF * (half + 1))
                    for r in range(PARTS):
                        sp.dma_start(tile[ROWS_OF_PART * r:ROWS_OF_PART * (r + 1), heads], src[:, heads])\
                            .then_inc(s_kstack[i][half], 16)

            xv = x.rearrange("b (t p) c -> p b t c", p=P)
            sp.dma_start(x_sb[:, 0], xv[:, 0]).then_inc(s_x[0], 16)
            sp.dma_start(first_sb[:], first).then_inc(s_first, 16)
            sp.dma_start(x_sb[:, 1], xv[:, 1]).then_inc(s_x[1], 16)
            sp.dma_start(ctxw_sb[:], ctxw).then_inc(s_ctxw, 16)
            sp.dma_start(Ks[0][SLOT_ROWS:ROWS], k_fixed).then_inc(s_fixed[0], 16)
            sp.dma_start(Qs[0][SLOT_ROWS:ROWS], q_fixed).then_inc(s_fixed[0], 16)
            sp.dma_start(late_sb[:], late).then_inc(s_late, 16)
            sp.dma_start(rows_sb[:], rows.partition_broadcast(P)).then_inc(s_late, 16)
            write_k(0, k_scr[0], S)
            write_q(0)
            for half in range(2):
                read_k(0, Ks[0], k_scr[0], [half])
                read_q(0, 0, [half])
            write_q(1)
            sp.dma_start(Ks[1][SLOT_ROWS:ROWS], k_fixed).then_inc(s_fixed[1], 16)
            sp.dma_start(Qs[1][SLOT_ROWS:ROWS], q_fixed).then_inc(s_fixed[1], 16)
            write_k(1, k_scr[1], S)

            def second_batch(i):
                if i == 0:
                    read_q(1, 1)
                else:
                    read_k(1, Ks[1], k_scr[1])

            def negmax(n):
                kind, b, g = GROUPS[n]
                sp.wait_ge(s_nmT, n + 1)
                sp.dma_start(Qs[b][MAXROW:ROWS, G * g:G * g + G], nmT[n % 2][:]).then_inc(s_nmrow[n % 2], 16)

            def context_keys():
                sp.dma_start(K2s[SLOT_ROWS:ROWS], k2_fixed).then_inc(s_fixed2, 16)
                write_k(2, k2_scr, B * MP)
                read_k(2, K2s, k2_scr)

            def weights(i):
                if i == 0:
                    sp.wait_ge(s_st, ST_FIRST[B * NG])
                tile, src = ((mw1_sb, mw1), (mw2_sb, mw2))[i // 2]
                half = slice(i % 2 * (E // 2), (i % 2 + 1) * (E // 2))
                sp.dma_start(tile[:, half], src[:, half]).then_inc(s_moew, 16)

            def finish(b):
                sp.wait_ge(s_fin, b + 1)
                sp.dma_start(out.rearrange("b (t p) c -> p b t c", p=P)[:, b], x_sb[:, b]).then_inc(s_out, 16)

            play({"negrow": negmax, "q2parts": lambda b: write_q(B + b),
                  "q2read": lambda b: read_q(B + b, b), "finish": finish,
                  "second_batch": second_batch, "context_keys": context_keys, "weights": weights})
            sp.wait_ge(s_out, 16 * B)

        @block.gpsimd
        def _(pool):
            links = 0

            def link(ins):
                nonlocal links
                links += 1
                ins.then_inc(s_pool, 1)
                pool.wait_ge(s_pool, links)

            def rstd_of(n, b):
                pool.wait_ge(s_var, n + 1)
                pool.tensor_tensor(rstd[:, NT * b:NT * b + NT], veps[:, NT * b:NT * b + NT], neghalf[:],
                                   ALU.pow).then_inc(s_rstd, 1)

            link(pool.memset(neghalf[:], -0.5))
            pool.memset(V2s[:], 0.0).then_inc(s_vpad, 1)
            pool.memset(Vs[0][:], 0.0).then_inc(s_vpad, 1)
            rstd_of(0, 0)
            link(pool.memset(maskb[:], 0.0))
            pool.affine_select(out=maskb[:], in_=maskb[:], compare_op=ALU.is_ge, fill=-1e30, base=0,
                               pattern=[[-1, P]], channel_multiplier=1).then_inc(s_const, 1)
            pool.wait_ge(s_vpad, 2)
            pool.memset(V2s[:, :, :, HD:HD + 1], 1.0).then_inc(s_vpad, 1)
            pool.memset(Vs[0][:, :, :, HD:HD + 1], 1.0).then_inc(s_vpad, 1)
            rstd_of(1, 1)
            pool.memset(Vs[1][:], 0.0).then_inc(s_vpad, 1)
            pool.wait_ge(s_vpad, 5)
            pool.memset(Vs[1][:, :, :, HD:HD + 1], 1.0).then_inc(s_vpad, 1)
            for i, width in ((1, S), (2, B * MP)):
                pool.wait_ge(s_kfull, i + 1)
                if i == 2:
                    pool.wait_ge(s_kscr, 16)
                split(pool, link, kparts[i % 2][:, :, 0:width], full[2][:] if i == 1 else full_k2, rest[2][:, 0:width])\
                    .then_inc(s_kparts[i], 1)
                pool.wait_ge(s_kparts[i], 1)
            link(pool.memset(ones[:], 1.0))

            def scores(n, i):
                if KIND(n) == "cross":
                    return
                at, width, blocks = exp_units("self")[i]
                pool.wait_ge(s_exp, ST_FIRST[n] + i + 1)
                nb = len(blocks)
                if nb == 1:
                    v = prob[n % 2][:, at:at + P].unsqueeze(1)
                else:
                    step = blocks[1][2]
                    v = prob[n % 2][:, at:at + S].rearrange("p (n s) -> p n s", s=P)[:, 0:step // P + 1:step // P, :]
                pool.affine_select(out=v, in_=v, compare_op=ALU.is_ge, fill=0.0, base=0,
                                   pattern=[[0, nb], [1, P]], channel_multiplier=-1).then_inc(s_causal, 1)

            def reciprocal_deviation(i):
                b = i % B
                rstd_of(B + i, b)
                if i < B:
                    if i == 0:
                        pool.wait_ge(s_late, 32)
                    pool.wait_ge(s_centred, i + 1)
                    pool.tensor_tensor(x_sb[:, b], x_sb[:, b], b2_sb.unsqueeze(1).to_broadcast([P, NT, C]), ALU.add)\
                        .then_inc(s_b2, 1)

            def split_tokens(ln, b):
                if ln == 2:
                    pool.wait_ge(s_norm, B + b + 1)
                    split(pool, link, xns[b], xn[:, b], rest[2][:].rearrange("p (t c) -> p t c", t=NT))\
                        .then_inc(s_xns, 1)

            def split_probs(b):
                pool.wait_ge(s_pr, b + 1)
                split(pool, link, prs[b], pr[b][:], pr_rest[:]).then_inc(s_prs, 1)

            def experts_out(k):
                pool.wait_ge(s_yhi, k + 1)
                pool.tensor_tensor(ys[k % 2][:, 1], yf[k % 2], ys[k % 2][:, 0], ALU.subtract).then_inc(s_y, 1)

            play({"experts_out": experts_out, "scores": scores, "xnT": split_tokens, "choice": split_probs,
                  "norm": reciprocal_deviation})

        @block.scalar
        def _(act):
            def copy_xnT(i, b, bank):
                act.wait_ge(s_xnTp, i + 1)
                act.copy(xnT[:, b], bank[:]).then_inc(s_xnT, 1)

            def copy_values(b):
                act.wait_ge(s_vp, b + 1)
                act.wait_ge(s_vpad, 4 + 2 * b)
                act.copy(Vs[b][:, :, :, 0:HD], v_banks[b][:].rearrange("p (t h d) -> p t h d", t=NT, d=HD))\
                    .then_inc(s_v, 1)

            def scale_queries(b):
                act.wait_ge(s_qp, b + 1)
                act.activation(full[3 * b][:], q_banks[b][:], ACT.Copy, scale=SCALE).then_inc(s_qfull, 1)

            def copy_keys(i, width):
                act.wait_ge(s_kp, i + 1)
                if i < B:
                    act.copy(full[1 + i][:, 0:width], k_banks[i][:, 0:width]).then_inc(s_kfull, 1)
                else:
                    act.activation(full_k2, k_banks[i][:, 0:width], ACT.Identity, bias=bk_sb[:, 0:1])\
                        .then_inc(s_kfull, 1)

            for b in range(B):
                copy_xnT(b, b, ps[2 + b])
                copy_keys(b, S)
                scale_queries(b)
                copy_values(b)
            act.wait_ge(s_vp, 3)
            for b in range(B):
                act.copy(V2s[:, b, :, 0:HD], v_banks[2][0:M, b * C:(b + 1) * C].rearrange("p (h d) -> p h d", d=HD))\
                    .then_inc(s_v, 1)
            act.wait_ge(s_late, 32)
            copy_keys(2, B * MP)

            def negmax_out(n):
                act.wait_ge(s_nmTp, n + 1)
                if n >= 2:
                    act.wait_ge(s_nmrow[n % 2], 16 * (n // 2))
                act.copy(nmT[n % 2][:], tp_bank[:].bitcast(BF16)[0:2 * G, 0:S]).then_inc(s_nmT, 1)

            def scores(n, i):
                rows = P if KIND(n) == "self" else M
                at, width, blocks = exp_units(KIND(n))[i]
                seq = ST_FIRST[n] + i
                act.wait_ge(s_st, seq + 1)
                if n >= 2:
                    act.wait_ge(s_pv, n - 1)
                act.activation(prob[n % 2][0:rows, at:at + width], st_banks[seq % STB][0:rows, 0:width],
                               ACT.Exp).then_inc(s_exp, 1)

            def values_out(n):
                act.wait_ge(s_pv, n + 1)
                if n >= 2:
                    act.wait_ge(s_oTp, n - 1)
                act.copy(oT[n % 2][:], pv_bank[:]).then_inc(s_oT, 1)

            def copy_onT(i):
                act.wait_ge(s_onTp, i + 1)
                act.copy(onT[i % B][:], tail_bank[:]).then_inc(s_onT, 1)

            def scale_tokens(i):
                b = i % B
                act.wait_ge(s_centred, i + 1)
                act.wait_ge(s_rstd, B + i + 1)
                for t in range(NT):
                    ins = act.activation(xn[:, b, t], xn[:, b, t], ACT.Copy, scale=rstd[:, NT * b + t:NT * b + t + 1])
                ins.then_inc(s_norm, 1)

            def hidden_mlp(b, j):
                act.wait_ge(s_h1p, 2 * b + j + 1)
                act.activation(h1[b][:, j], tail_bank[:], ACT.Relu, bias=b1_sb[:, j:j + 1]).then_inc(s_h1, 1)

            def gate(b):
                act.wait_ge(s_gz, b + 1)
                act.activation(pr[b][:], pr[b][:], ACT.Exp).then_inc(s_gexp, 1)

            def choice(b):
                act.wait_ge(s_prT, b + 1)
                act.copy(work[b], tail_bank[0:E, :]).then_inc(s_work, 1)

            def gather(k):
                act.wait_ge(s_gather, k + 1)
                if k >= 2:
                    act.wait_ge(s_hid, k - 1)
                act.copy(xin[k % 2], gather_banks[k % 2][:, 0:CAP]).then_inc(s_xin, 1)

            def turn(k):
                act.wait_ge(s_turn, k + 1)
                if k >= 2:
                    act.wait_ge(s_comb, k - 1)
                act.copy(scatter[k % 2][:], turn_bank[:].bitcast(BF16)[:, 0:S]).then_inc(s_scatter, 1)

            def experts_hidden(k):
                act.wait_ge(s_hid, k + 1)
                if k >= 2:
                    act.wait_ge(s_yp, k - 1)
                act.activation(hidden[k % 2], hid_banks[k % 2][:], ACT.Gelu).then_inc(s_gelu, 1)

            def experts_out(k):
                act.wait_ge(s_yp, k + 1)
                act.wait_ge(s_pslot, k + 1)
                if k >= 2:
                    act.wait_ge(s_comb, k - 1)
                act.activation(yf[k % 2], y_bank[:, 0:C], ACT.Copy, scale=pslot[k % 2][:, 0:1])
                act.activation(ys[k % 2][:, 0], y_bank[:, 0:C], ACT.Copy, scale=pslot[k % 2][:, 0:1])\
                    .then_inc(s_yhi, 1)

            def gathered(b):
                act.wait_ge(s_comb, E * (b + 1))
                act.copy(combT[b][:], comb_bank[:]).then_inc(s_combT, 1)

            play({"negrow": negmax_out, "choice": choice, "onT": copy_onT, "norm": scale_tokens, "combined": gathered, "scores": scores,
                  "values_out": values_out,
                  "xnT": lambda ln, b: copy_xnT(B * ln + b, b, tail_bank), "hidden": hidden_mlp, "gate": gate,
                  "gather": gather, "turn": turn, "experts_hidden": experts_hidden, "experts_out": experts_out})

        @block.vector
        def _(dve):
            links = 0

            def link(ins):
                nonlocal links
                links += 1
                ins.then_inc(s_dve, 1)
                dve.wait_ge(s_dve, links)

            def statistics(b):
                for t in range(NT):
                    ins = dve.bn_stats(stats[:, t], x_sb[:, b, t])
                link(ins)
                for t in range(NT):
                    ins = dve.bn_aggr(mv[:, NT * b + t], stats[:, t])
                link(ins)
                dve.tensor_scalar(veps[:, NT * b:NT * b + NT], mv[:, NT * b:NT * b + NT, 1], EPS, None, ALU.add)\
                    .then_inc(s_var, 1)

            def normalise_tokens(n, b):
                dve.wait_ge(s_rstd, n + 1)
                for t in range(NT):
                    i = NT * b + t
                    ins = dve.tensor_scalar(xn[:, b, t], x_sb[:, b, t], mv[:, i, 0:1], rstd[:, i:i + 1],
                                            ALU.subtract, ALU.mult)
                ins.then_inc(s_xn, 1)
                dve.wait_ge(s_xn, n + 1)

            def split_queries(i, value):
                if i >= B:
                    dve.wait_ge(s_qscr, 16 * (i - 1))
                split(dve, link, qparts[i % 2], value, rest[0][:]).then_inc(s_qparts, 1)

            def cross_queries(b):
                dve.wait_ge(s_qp, B + b + 1)
                dve.tensor_scalar(full[0][:], tail_bank[:], bq_sb[:, 0:1], SCALE, ALU.add, ALU.mult)\
                    .then_inc(s_q2full, 1)
                dve.wait_ge(s_q2full, b + 1)
                split_queries(B + b, full[0][:])

            dve.wait_ge(s_x[0], 16)
            statistics(0)
            normalise_tokens(0, 0)
            dve.wait_ge(s_first, 16)
            dve.tensor_copy(identb[:], ident_sb).then_inc(s_identb, 1)
            dve.wait_ge(s_x[1], 16)
            statistics(1)
            normalise_tokens(1, 1)
            dve.wait_ge(s_kfull, 1)
            split(dve, link, kparts[0], full[1][:], rest[1][:]).then_inc(s_kparts[0], 1)
            for b in range(B):
                dve.wait_ge(s_qfull, b + 1)
                split_queries(b, full[3 * b][:])
            dve.wait_ge(s_v, 2 * B)
            dve.wait_ge(s_late, 32)
            for b in range(B):
                v = V2s[:, b, :, 0:HD]
                dve.tensor_tensor(v, v, bv_sb.rearrange("p (h d) -> p h d", d=HD), ALU.add).then_inc(s_v2, 1)

            def maxima(n, i):
                t, heads, keys = max_units(KIND(n))[i]
                seq = MX_FIRST[n] + i
                dve.wait_ge(s_mx, seq + 1)
                bank = mx_banks[seq % MXB][:, 0:len(heads) * keys].rearrange("p (h k) -> p h k", k=keys)
                dve.tensor_reduce(nmax[n % 2][:, t, heads[0]:heads[0] + len(heads)], bank, AX.X, ALU.max,
                                  negate=True).then_inc(s_mxfree, 1)

            def negmax(n):
                dve.wait_ge(s_mxfree, MX_FIRST[n + 1])
                if n >= 2:
                    dve.wait_ge(s_nmTp, n - 1)
                link(dve.tensor_copy(nmp[n % 2][:, :, 0, :], nmax[n % 2][:]))
                dve.tensor_tensor(nmp[n % 2][:, :, 1, :], nmax[n % 2][:], nmp[n % 2][:, :, 0, :], ALU.subtract)\
                    .then_inc(s_nmp, 1)

            def output(n):
                kind, b, g = GROUPS[n]
                dve.wait_ge(s_oTp, n + 1)
                tp = tp_bank[:].rearrange("p (t h w) -> p t h w", t=NT, w=VW)
                link(dve.reciprocal(rden[:], tp[:, :, :, HD]))
                w = G * HD
                o = on[b][:, :, w * g:w * g + w].rearrange("p t (h d) -> p t h d", d=HD)
                dve.tensor_tensor(o, tp[:, :, :, 0:HD], rden[:].unsqueeze(3).to_broadcast([P, NT, G, HD]),
                                  ALU.mult).then_inc(s_on, 1)
                dve.wait_ge(s_on, n + 1)

            def add_residual(i, b):
                dve.wait_ge(s_resp, i + 1)
                if i >= B:
                    dve.wait_ge(s_b2, i - B + 1)
                xb = x_sb[:, b].rearrange("p t c -> p (t c)")
                dve.tensor_tensor(xb, tail_bank[:], xb, ALU.add).then_inc(s_res, 1)
                dve.wait_ge(s_res, i + 1)
                statistics(b)
                for t in range(NT):
                    ins = dve.tensor_scalar(xn[:, b, t], x_sb[:, b, t], mv[:, NT * b + t, 0:1], None, ALU.subtract)
                ins.then_inc(s_centred, 1)

            def gate(b):
                dve.wait_ge(s_gate, b + 1)
                z = tail_bank[:, 0:NT * E].rearrange("p (n e) -> p n e", e=E)
                link(dve.tensor_reduce(gmax[:], z, AX.X, ALU.max))
                dve.tensor_tensor(pr[b][:], z, gmax[:].unsqueeze(2).to_broadcast([P, NT, E]), ALU.subtract)\
                    .then_inc(s_gz, 1)

            def probs(b):
                dve.wait_ge(s_gexp, b + 1)
                link(dve.tensor_reduce(gsum[:], pr[b][:], AX.X, ALU.add))
                link(dve.reciprocal(gsum[:], gsum[:]))
                dve.tensor_tensor(pr[b][:], pr[b][:], gsum[:].unsqueeze(2).to_broadcast([P, NT, E]), ALU.mult)\
                    .then_inc(s_pr, 1)
                dve.wait_ge(s_pr, b + 1)

            def top(b, r):
                if r == 0:
                    dve.wait_ge(s_work, b + 1)
                link(dve.max(top8[:], work[b]))
                link(dve.match_replace(work[b], top8[:], work[b], -1.0))

            def slots(b):
                link(dve.tensor_scalar(sel[b], work[b], 0.0, None, ALU.is_lt))
                link(dve.tensor_tensor_scan(slot[b], sel[b], ones[:], 0.0, ALU.add, ALU.mult))
                dve.tensor_tensor(slot[b], slot[b], sel[b], ALU.mult).then_inc(s_slot, 1)

            def slotsT(b):
                dve.wait_ge(s_slotT, b + 1)
                dve.tensor_copy(slT[b][:], tail_bank[:, 0:NT * E].rearrange("p (t n) -> p t n", t=NT))\
                    .then_inc(s_slT, 1)
                dve.wait_ge(s_slT, b + 1)

            def choose(k):
                b, e = divmod(k, E)
                if e == 0:
                    dve.wait_ge(s_slT, b + 1)
                if k >= 2:
                    dve.wait_ge(s_turn, k - 1)
                dve.tensor_tensor(onehot[k % 2][:], iota_sb.unsqueeze(1).to_broadcast([P, NT, CAP]),
                                  slT[b][:, :, e:e + 1].to_broadcast([P, NT, CAP]), ALU.is_equal)\
                    .then_inc(s_onehot, 1)

            def gather(k):
                dve.wait_ge(s_xin, k + 1)
                bank = gather_banks[k % 2]
                if k >= 2:
                    dve.wait_ge(s_yhi, k - 1)
                dve.tensor_reduce(pslot[k % 2][:], bank[:, CAP:CAP + PARTS], AX.X, ALU.add).then_inc(s_pslot, 1)

            def finish(b):
                dve.wait_ge(s_combTp, b + 1)
                xb = x_sb[:, b].rearrange("p t c -> p (t c)")
                dve.tensor_tensor(xb, tail_bank[:], xb, ALU.add).then_inc(s_fin, 1)

            play({"max": maxima, "negmax": negmax, "output": output, 
                  "sum": lambda i: add_residual(i, i % B),
                  "q2parts": cross_queries,
                  "gate": gate, "probs": probs,
                  "top": top, "slots": slots, "slotsT": slotsT, "choose": choose,
                  "gather": gather, "finish": finish})

        @block.tensor
        def _(pe):
            def transposed(bank, tiles):
                for t in range(NT):
                    src = tiles(t)
                    ins = pe.transpose(bank[0:src.shape[1], t * P:t * P + P], src, ident_sb)
                return ins

            pe.wait_ge(s_first, 16)
            for b in range(B):
                pe.wait_ge(s_xn, b + 1)
                transposed(ps[2 + b], lambda t: xn[:, b, t]).then_inc(s_xnTp, 1)
                pe.wait_ge(s_xnT, b + 1)
                pe.matmul(k_banks[b][:], wqkvT_sb[:, C:2 * C], xnT[:, b], start=True, stop=True).then_inc(s_kp, 1)
                pe.matmul(q_banks[b][:], wqkvT_sb[:, 0:C], xnT[:, b], start=True, stop=True).then_inc(s_qp, 1)
                for t in range(NT):
                    ins = pe.matmul(v_banks[b][:, t * C:(t + 1) * C], xnT[:, b, t * P:(t + 1) * P],
                                    wqkvT_sb[:, 2 * C:3 * C], start=True, stop=True)
                ins.then_inc(s_vp, 1)
            pe.wait_ge(s_ctxw, 16)
            pe.wait_ge(s_v, 1)
            for b in range(B):
                ins = pe.matmul(v_banks[2][0:M, b * C:(b + 1) * C], ctxT_sb[:, MP * b:MP * b + M], wv_sb, start=True,
                                stop=True)
            ins.then_inc(s_vp, 1)
            pe.wait_ge(s_kfull, 1)
            pe.matmul(k_banks[2][:, 0:B * MP], wk_sb, ctxT_sb, start=True, stop=True).then_inc(s_kp, 1)
            pe.wait_ge(s_const, 1)
            pe.wait_ge(s_identb, 1)
            pe.wait_ge(s_xnT, B)
            pe.wait_ge(s_v, 2 * B)
            pe.wait_ge(s_kfull, 3)
            pe.wait_ge(s_qfull, B)

            def operands(n):
                kind, b, g = GROUPS[n]
                if kind == "self":
                    return Qs[b][0:ROWS, G * g:G * g + G], Ks[b][0:ROWS, G * g:G * g + G]
                return Qs[b][0:ROWS, G * g:G * g + G], K2s[0:ROWS, G * g:G * g + G, MP * b:MP * b + M]

            def max_scores(n, i):
                kind, b, g = GROUPS[n]
                q, k = operands(n)
                t, heads, keys = max_units(kind)[i]
                seq = MX_FIRST[n] + i
                if i == 0:
                    if kind == "self":
                        pe.wait_ge(s_qstack[b][g // 2], 16 * PARTS)
                        pe.wait_ge(s_kstack[b][g // 2], 16 * PARTS)
                        pe.wait_ge(s_fixed[b], 32)
                    else:
                        pe.wait_ge(s_qstack[B + b][g // 2], 16 * PARTS)
                        pe.wait_ge(s_kstack[B][g // 2], 16 * PARTS)
                        pe.wait_ge(s_fixed2, 16)
                if seq >= MXB:
                    pe.wait_ge(s_mxfree, seq - MXB + 1)
                bank = mx_banks[seq % MXB]
                for j, h in enumerate(heads):
                    ins = pe.matmul(bank[:, j * keys:(j + 1) * keys], q[0:MAXROW, h, t * P:(t + 1) * P],
                                    k[0:MAXROW, h, 0:keys], start=(j == 0), stop=(kind == "cross"),
                                    skip_group_check=True)
                    if kind == "self":
                        ins = pe.matmul(bank[:, (j + 1) * keys - P:(j + 1) * keys], identb[:], maskb[:],
                                        start=False, stop=True, skip_group_check=True)
                ins.then_inc(s_mx, 1)

            def negmax(n):
                pe.wait_ge(s_nmp, n + 1)
                take("outputs", (s_nmT, n + 1))
                for t in range(NT):
                    ins = pe.transpose(tp_bank[:].bitcast(BF16)[0:2 * G, t * P:(t + 1) * P],
                                       nmp[n % 2][:, t].rearrange("p i h -> p (i h)"), identb[:])
                ins.then_inc(s_nmTp, 1)

            def scores(n, i):
                kind, b, g = GROUPS[n]
                q, k = operands(n)
                at, width, blocks = exp_units(kind)[i]
                seq = ST_FIRST[n] + i
                if i == 0:
                    pe.wait_ge(s_nmrow[n % 2], 16 * (n // 2 + 1))
                if seq >= STB:
                    pe.wait_ge(s_exp, seq - STB + 1)
                for m, (h, j, col, qt) in enumerate(blocks):
                    rows, keys = (P, k[:, h, j * P:(j + 1) * P]) if kind == "self" else (M, k[:, h, :])
                    ins = pe.matmul(st_banks[seq % STB][0:rows, col:col + S - qt * P], keys, q[:, h, qt * P:S],
                                    start=(m == 0), stop=True, skip_group_check=True)
                ins.then_inc(s_st, 1)

            def values(n, j):
                kind, b, g = GROUPS[n]
                if j == 0:
                    if kind == "cross":
                        pe.wait_ge(s_exp, ST_FIRST[n + 1])
                        pe.wait_ge(s_v2, B)
                    if n > 0:
                        pe.wait_ge(s_oT, n)
                if kind == "self":
                    last_unit = max(u for u, (_, _, bl) in enumerate(exp_units(kind)) if j in [blk[1] for blk in bl])
                    pe.wait_ge(s_causal, ST_FIRST[n] + last_unit + 1)
                last = NT - 1 if kind == "self" else 0
                for h, at, qt in sorted((h, at + col, qt) for at, _, bl in exp_units(kind) for h, jj, col, qt in bl
                                        if jj == j):
                    v, rows = (Vs[b][:, j, G * g + h, :], P) if kind == "self" else (V2s[:, b, G * g + h, :], M)
                    ins = pe.matmul(pv_bank[VW * h:VW * h + VW, qt * P:S], v,
                                    prob[n % 2][0:rows, at:at + S - qt * P], start=(j == 0), stop=(j == last),
                                    tile_position=(0, VW * h), skip_group_check=True)
                if j == last:
                    ins.then_inc(s_pv, 1)

            users = {}

            def take(bank, user):
                if bank in users:
                    pe.wait_ge(*users[bank])
                users[bank] = user

            def output(n):
                pe.wait_ge(s_oT, n + 1)
                take("outputs", (s_on, n + 1))
                transposed(tp_bank, lambda t: oT[n % 2][:, t * P:(t + 1) * P]).then_inc(s_oTp, 1)

            def turn_on(i):
                pe.wait_ge(s_on, NG * (i + 1))
                take("tail", (s_onT, i + 1))
                transposed(tail_bank, lambda t: on[i % B][:, t]).then_inc(s_onTp, 1)

            def residual(b):
                pe.wait_ge(s_late, 32)
                pe.wait_ge(s_onT, b + 1)
                take("tail", (s_res, b + 1))
                for t in range(NT):
                    ins = pe.matmul(tail_bank[:, t * C:(t + 1) * C], onT[b][:, t * P:(t + 1) * P], woT_sb, start=True,
                                    stop=True)
                ins.then_inc(s_resp, 1)

            def turn_xn(ln, b):
                i = B * ln + b
                pe.wait_ge(s_norm, i - B + 1)
                take("tail", (s_xnT, i + 1))
                transposed(tail_bank, lambda t: xn[:, b, t]).then_inc(s_xnTp, 1)

            def q2(b):
                pe.wait_ge(s_xnT, B + b + 1)
                take("tail", (s_q2full, b + 1))
                pe.matmul(tail_bank[:], wq_sb, xnT[:, b], start=True, stop=True).then_inc(s_qp, 1)

            def hidden_mlp(b, j):
                pe.wait_ge(s_onT, B + b + 1)
                take("tail", (s_h1, 2 * b + j + 1))
                pe.matmul(tail_bank[:], w1_sb[:, j * C:(j + 1) * C], onT[b][:], start=True, stop=True)\
                    .then_inc(s_h1p, 1)

            def mlp(b):
                pe.wait_ge(s_h1, 2 * b + 2)
                take("tail", (s_res, B + b + 1))
                for t in range(NT):
                    for j in range(2):
                        ins = pe.matmul(tail_bank[:, t * C:(t + 1) * C], h1[b][:, j, t * P:(t + 1) * P],
                                        w2_sb[:, j * C:(j + 1) * C], start=(j == 0), stop=(j == 1),
                                        skip_group_check=True)
                ins.then_inc(s_resp, 1)

            def gate(b):
                pe.wait_ge(s_xnT, 2 * B + b + 1)
                take("tail", (s_gz, b + 1))
                for t in range(NT):
                    ins = pe.matmul(tail_bank[:, t * E:(t + 1) * E], xnT[:, b, t * P:(t + 1) * P], gw_sb, start=True,
                                    stop=True)
                ins.then_inc(s_gate, 1)

            def choice(b):
                pe.wait_ge(s_pr, b + 1)
                take("tail", (s_work, b + 1))
                transposed(tail_bank, lambda t: pr[b][:, t]).then_inc(s_prT, 1)

            def slots(b):
                pe.wait_ge(s_slot, b + 1)
                take("tail", (s_slT, b + 1))
                for t in range(NT):
                    ins = pe.transpose(tail_bank[:, t * E:(t + 1) * E], slot[b][:, t * P:(t + 1) * P],
                                       ident_sb[0:E, 0:E])
                ins.then_inc(s_slotT, 1)

            def gather(k):
                b, e = divmod(k, E)
                pe.wait_ge(s_onehot, k + 1)
                pe.wait_ge(s_xns, b + 1)
                pe.wait_ge(s_prs, b + 1)
                if k >= 2:
                    pe.wait_ge(s_pslot, k - 1)
                    pe.wait_ge(s_xin, k - 1)
                bank = gather_banks[k % 2]
                for t in range(NT):
                    for i in range(PARTS):
                        pe.matmul(bank[:, 0:CAP], xns[b][:, i, t], onehot[k % 2][:, t], start=(t == 0 and i == 0),
                                  stop=(t == NT - 1 and i == PARTS - 1), skip_group_check=True)
                for t in range(NT):
                    ins = pe.matmul(bank[:, CAP:CAP + PARTS], onehot[k % 2][:, t], prs[b][:, :, t, e],
                                    start=(t == 0), stop=(t == NT - 1), skip_group_check=True)
                ins.then_inc(s_gather, 1)

            def turn(k):
                if k >= 1:
                    pe.wait_ge(s_scatter, k)
                for t in range(NT):
                    ins = pe.transpose(turn_bank[:].bitcast(BF16)[:, t * P:(t + 1) * P], onehot[k % 2][:, t],
                                       identb[:])
                ins.then_inc(s_turn, 1)

            def experts_hidden(k):
                b, e = divmod(k, E)
                if k == 0:
                    pe.wait_ge(s_moew, 64)
                pe.wait_ge(s_xin, k + 1)
                if k >= 2:
                    pe.wait_ge(s_gelu, k - 1)
                for c in range(NC):
                    ins = pe.matmul(hid_banks[k % 2][:, c * CAP:(c + 1) * CAP], mw1_sb[:, e, c * P:(c + 1) * P],
                                    xin[k % 2], start=(c == 0), stop=True, skip_group_check=True)
                ins.then_inc(s_hid, 1)

            def experts_out(k):
                b, e = divmod(k, E)
                pe.wait_ge(s_gelu, k + 1)
                if k >= 1:
                    pe.wait_ge(s_yhi, k)
                for c in range(NC):
                    ins = pe.matmul(y_bank[:, 0:C], hidden[k % 2][:, c * CAP:(c + 1) * CAP], mw2_sb[:, e, c],
                                    start=(c == 0), stop=(c == NC - 1))
                ins.then_inc(s_yp, 1)

            def combine(k):
                b, e = divmod(k, E)
                pe.wait_ge(s_y, k + 1)
                pe.wait_ge(s_scatter, k + 1)
                if e == 0 and b:
                    pe.wait_ge(s_combT, b)
                for i in range(2):
                    ins = pe.matmul(comb_bank[:], ys[k % 2][:, i], scatter[k % 2][:], start=(e == 0 and i == 0),
                                    stop=(e == E - 1 and i == 1))
                ins.then_inc(s_comb, 1)

            def finish(b):
                pe.wait_ge(s_combT, b + 1)
                take("tail", (s_fin, b + 1))
                transposed(tail_bank, lambda t: combT[b][:, t * P:(t + 1) * P]).then_inc(s_combTp, 1)

            play({"finish": finish, "max": max_scores, "negrow": negmax, "scores": scores, "values": values,
                  "output": output,
                  "onT": turn_on, "residual": residual, "xnT": turn_xn, "q2": q2, "hidden": hidden_mlp, "mlp": mlp,
                  "gate": gate, "choice": choice, "slotsT": slots, "gather": gather, "turn": turn,
                  "experts_hidden": experts_hidden, "experts_out": experts_out, "combine": combine})



def bf16_parts(v):
    out = []
    for _ in range(PARTS):
        hi = (v.view(np.uint32) & np.uint32(0xFFFF0000)).view(np.float32)
        out.append((hi.view(np.uint32) >> 16).astype(np.uint16))
        v = (v - hi).astype(np.float32)
    return np.stack(out)


def fixed_rows(rows, width):
    out = np.zeros((ROWS - SLOT_ROWS, H, width), np.uint16)
    for row, bits in rows:
        out[row - SLOT_ROWS] = bits
    return out


def shape_constants():
    slopes = np.float32([(2.0 ** -0.5) ** (i + 1) for i in range(H)])
    alibi = bf16_parts(np.ascontiguousarray(-(slopes[:, None] * np.arange(S, dtype=np.float32)[None, :])))
    one = np.uint16(0x3F80)
    return {
        "k_fixed": fixed_rows([(ALIBI + i, alibi[i]) for i in range(PARTS)] + [(MAXROW, one), (MAXROW + 1, one)], S),
        "q_fixed": fixed_rows([(ALIBI + i, one) for i in range(PARTS)], S),
        "k2_fixed": fixed_rows([(MAXROW, one), (MAXROW + 1, one)], B * MP),
    }


def kernel(x, ctx_768, L0_attn_W_qkv, L0_attn_W_o, L0_xattn_Wq, L0_xattn_bq, L0_xattn_Wk, L0_xattn_bk,
           L0_xattn_Wv, L0_xattn_bv, L0_xattn_W1, L0_xattn_b1, L0_xattn_W2, L0_xattn_b2, L0_ffn_gate_w,
           L0_ffn_w1, L0_ffn_w2):
    import concourse.bacc as bacc
    from concourse.bass_utils import run_bass_kernel_spmd

    a = np.asarray

    def channel_first(w):
        return w.reshape(w.shape[0], H, HD).transpose(0, 2, 1).reshape(w.shape[0], C)

    wqkvT = a(L0_attn_W_qkv).T
    padded = np.zeros((CT, B, MP), np.float32)
    padded[:, :, 0:M] = a(ctx_768).transpose(2, 0, 1)
    iota = np.broadcast_to(np.arange(1, P + 1, dtype=np.float32), (P, P))
    data = {
        "x": a(x),
        "first": np.concatenate([channel_first(wqkvT[:, 0:C]), channel_first(wqkvT[:, C:2 * C]),
                                 wqkvT[:, 2 * C:], np.eye(P, dtype=np.float32)], axis=1),
        "ctxw": np.concatenate([channel_first(a(L0_xattn_Wk)), a(L0_xattn_Wv), padded.reshape(CT, B * MP)], axis=1),
        "late": np.concatenate([
            a(L0_attn_W_o).T, channel_first(a(L0_xattn_Wq)), a(L0_xattn_W1),
            a(L0_xattn_W2).reshape(2, C, C).transpose(1, 0, 2).reshape(C, 2 * C), iota,
            a(L0_xattn_b1).reshape(2, C).T, channel_first(a(L0_xattn_bq)[None]).T,
            channel_first(a(L0_xattn_bk)[None]).T, a(L0_ffn_gate_w)], axis=1),
        "rows": np.concatenate([a(L0_xattn_bv), a(L0_xattn_b2)]),
        "mw1": a(L0_ffn_w1).transpose(1, 0, 2),
        "mw2": a(L0_ffn_w2).reshape(E, NC, P, C).transpose(2, 0, 1, 3),
        **shape_constants(),
    }
    nc = bacc.Bacc("TRN2", target_bir_lowering=False, num_devices=1)
    arrays, args = {}, {}
    for name, v in data.items():
        v = np.ascontiguousarray(v)
        arrays[f"in_{name}"] = v
        t = nc.dram_tensor(f"in_{name}", v.shape, mybir.dt.from_np(v.dtype), kind="ExternalInput").ap()
        args[name] = t.bitcast(BF16) if v.dtype == np.uint16 else t
    out = nc.dram_tensor("out", (B, S, C), F32, kind="ExternalOutput").ap()
    decoder_block(nc, out=out, **args)
    r = run_bass_kernel_spmd(nc, [arrays], core_ids=[0])
    return r.results[0]["out"]
```
